# Optimizing a Trainium2 kernel written in Bass

```python
import numpy as np
import jax
import jax.numpy as jnp

def _softmax(x, axis=-1):
    return jax.nn.softmax(x, axis=axis)
def _gelu(x):
    return jax.nn.gelu(x, approximate=True)
def _silu(x):
    return jax.nn.silu(x)
def _sigmoid(x):
    return jax.nn.sigmoid(x)
def _layernorm(x, axis=-1, eps=1e-5):
    m = jnp.mean(x, axis=axis, keepdims=True)
    v = jnp.var(x, axis=axis, keepdims=True)
    return (x - m) / jnp.sqrt(v + eps)
def _scatter_add(tgt, idx, src, axis=0):
    return tgt.at[idx].add(src)
def _segment_sum(src, seg, n):
    return jax.ops.segment_sum(src, seg, n)

kernel_name = 'mk_adj_preln_d2_adj_256_b60210'

def setup_inputs(seed: int = 0):
    np.random.seed(seed)
    _w = jnp.asarray
    def _rec_inputs():
        import jax
        import jax.numpy as jnp
        _gk = jax.random.key(seed)
        x = -0.0002928 + 1 * jax.random.normal(jax.random.fold_in(_gk, 1), (128, 128, 256), jnp.float32)
        _a = jax.random.bernoulli(jax.random.fold_in(_gk, 2), 0.125, (128, 128, 128))
        _a = jnp.logical_or(_a, jnp.swapaxes(_a, -1, -2))
        _a = jnp.logical_or(_a, jnp.eye(128, dtype=bool))
        adj = _a.astype(jnp.int32)
        return x, adj
    x, adj = _rec_inputs()
    def _L0_gnn_setup():
        import jax, jax.numpy as jnp
        import numpy as np
        OUT = 256
        NUM_LAYERS = 3

        def _gru_cell(inp, h, w_ih, w_hh, b_ih, b_hh):
            gi = inp @ w_ih.T + b_ih
            gh = h @ w_hh.T + b_hh
            i_r, i_z, i_n = jnp.split(gi, 3, axis=-1)
            h_r, h_z, h_n = jnp.split(gh, 3, axis=-1)
            r = jax.nn.sigmoid(i_r + h_r)
            z = jax.nn.sigmoid(i_z + h_z)
            n = jnp.tanh(i_n + r * h_n)
            return (1.0 - z) * n + z * h
        key = jax.random.key(seed)
        ks = jax.random.split(key, 8)
        B, N, D = (32, 512, 256)
        x = jax.random.normal(ks[0], (B, N, D), dtype=jnp.float32)
        adj = jax.random.randint(ks[1], (B, N, N), 0, 2, dtype=jnp.int32)
        s = 1.0 / np.sqrt(OUT)
        weight = jax.random.uniform(ks[2], (NUM_LAYERS, OUT, OUT), jnp.float32, -s, s)
        w_ih = jax.random.uniform(ks[3], (3 * OUT, OUT), jnp.float32, -s, s)
        w_hh = jax.random.uniform(ks[4], (3 * OUT, OUT), jnp.float32, -s, s)
        b_ih = jax.random.uniform(ks[5], (3 * OUT,), jnp.float32, -s, s)
        b_hh = jax.random.uniform(ks[6], (3 * OUT,), jnp.float32, -s, s)
        return {'x': x, 'adj': adj, 'weight': weight, 'w_ih': w_ih, 'w_hh': w_hh, 'b_ih': b_ih, 'b_hh': b_hh}
    _L0_gnn_all = _L0_gnn_setup()
    _L0_gnn_in = {k: v for k, v in _L0_gnn_all.items() if k in ('weight', 'w_ih', 'w_hh', 'b_ih', 'b_hh', )}
    del _L0_gnn_all

    def _L1_gnn_setup():
        import jax, jax.numpy as jnp
        import numpy as np
        B, N, F_IN, F_OUT = (8, 2048, 256, 256)
        ALPHA = 0.2
        key = jax.random.key(seed)
        k1, k2, k3, k4 = jax.random.split(key, 4)
        h = jax.random.normal(k1, (B, N, F_IN), dtype=jnp.float32)
        adj = jax.random.randint(k2, (B, N, N), 0, 2, dtype=jnp.int32)
        W = jax.random.normal(k3, (F_OUT, F_IN), dtype=jnp.float32) / np.sqrt(F_IN)
        a = jax.random.normal(k4, (1, 2 * F_OUT), dtype=jnp.float32) / np.sqrt(2 * F_OUT)
        return {'h': h, 'adj': adj, 'W': W, 'a': a}
    _L1_gnn_all = _L1_gnn_setup()
    _L1_gnn_in = {k: v for k, v in _L1_gnn_all.items() if k in ('W', 'a', )}
    del _L1_gnn_all

    return {
        "x": x,
        "adj": adj,
        "L0_gnn_weight": _L0_gnn_in["weight"],
        "L0_gnn_w_ih": _L0_gnn_in["w_ih"],
        "L0_gnn_w_hh": _L0_gnn_in["w_hh"],
        "L0_gnn_b_ih": _L0_gnn_in["b_ih"],
        "L0_gnn_b_hh": _L0_gnn_in["b_hh"],
        "L1_gnn_W": _L1_gnn_in["W"],
        "L1_gnn_a": _L1_gnn_in["a"],
    }

def reference(x, adj, L0_gnn_weight, L0_gnn_w_ih, L0_gnn_w_hh, L0_gnn_b_ih, L0_gnn_b_hh, L1_gnn_W, L1_gnn_a):
    import jax
    import jax.numpy as jnp
    def _L0_gnn_ref(x, adj, weight, w_ih, w_hh, b_ih, b_hh):
        import jax, jax.numpy as jnp
        import numpy as np
        OUT = 256
        NUM_LAYERS = 3

        def _gru_cell(inp, h, w_ih, w_hh, b_ih, b_hh):
            gi = inp @ w_ih.T + b_ih
            gh = h @ w_hh.T + b_hh
            i_r, i_z, i_n = jnp.split(gi, 3, axis=-1)
            h_r, h_z, h_n = jnp.split(gh, 3, axis=-1)
            r = jax.nn.sigmoid(i_r + h_r)
            z = jax.nn.sigmoid(i_z + h_z)
            n = jnp.tanh(i_n + r * h_n)
            return (1.0 - z) * n + z * h
        A = (adj != 0).astype(x.dtype)
        h = x
        L = weight.shape[0]
        for i in range(L):
            m = jnp.einsum('bnd,de->bne', h, weight[i])
            aggr = jnp.einsum('bst,bsd->btd', A, m)
            h = _gru_cell(aggr, h, w_ih, w_hh, b_ih, b_hh)
        return h

    def _L1_gnn_ref(h, adj, W, a):
        import jax, jax.numpy as jnp
        import numpy as np
        B, N, F_IN, F_OUT = (8, 2048, 256, 256)
        ALPHA = 0.2
        Wh = jnp.einsum('bnf,of->bno', h, W)
        Fo = Wh.shape[-1]
        a1 = a[0, :Fo]
        a2 = a[0, Fo:]
        s1 = Wh @ a1
        s2 = Wh @ a2
        e = jax.nn.leaky_relu(s1[:, :, None] + s2[:, None, :], negative_slope=ALPHA)
        mask = adj == 0
        e = jnp.where(mask, -jnp.inf, e)
        att = jax.nn.softmax(e, axis=-1)
        att = jnp.where(mask, 0.0, att)
        return jnp.einsum('bij,bjo->bio', att, Wh)

    h = jnp.maximum(_layernorm(x, axis=-1), 0.0)
    x = x + _L0_gnn_ref(h, adj, L0_gnn_weight, L0_gnn_w_ih, L0_gnn_w_hh, L0_gnn_b_ih, L0_gnn_b_hh)
    h = jnp.maximum(_layernorm(x, axis=-1), 0.0)
    x = x + _L1_gnn_ref(h, adj, L1_gnn_W, L1_gnn_a)
    return x


_drawn_inputs = setup_inputs


def setup_inputs(seed=0):
    import zlib

    import numpy as np

    out = dict(_drawn_inputs(seed))
    spreads = {}
    factors = {}
    for name, (base, spread) in spreads.items():
        noise = np.random.default_rng([zlib.crc32(name.encode()), seed]).standard_normal(out[name].shape)
        drawn = base * np.exp(spread * noise) if base else spread * noise
        out[name] = jnp.asarray(drawn.astype(out[name].dtype))
    for name, factor in factors.items():
        out[name] = (out[name] * factor).astype(out[name].dtype)
    return out
```

```python
from contextlib import ExitStack

import concourse.bass as bass
from concourse import mybir

F32 = mybir.dt.float32
F32R = mybir.dt.float32r
F16 = mybir.dt.float16
I32 = mybir.dt.int32
ALU = mybir.AluOpType
ACT = mybir.ActivationFunctionType
AX_X = mybir.AxisListType.X

P = 128
D = 256
KC = D // P
GROUP = 4
T = GROUP * P
LAYERS = 3
GATES = 3 * KC
ALPHA = 0.2
EPS = 1e-5
MASKED = -1e30
HSCALE = 2048.0

STEPS = ("hn0", "r0", "in0", "z0", "hn1", "r1", "in1", "z1")
SIDE = {
    (0, 0): [("residual", 1, 0, -1)],
    (0, 1): [("first_transpose", 1, 0, 0)],
    (0, 2): [("residual", 1, 1, -1)],
    (0, 3): [("first_transpose", 1, 1, 0)],
    (0, 4): [("neighbours", 1, 0, 0, 0)],
    (0, 5): [("neighbours", 1, 0, 1, 0), ("att_transpose", 0, 0, -1)],
    (0, 6): [("stats_att", 1, -1)],
    (0, 7): [("att_transpose", 0, 1, -1)],
    (1, 0): [("transpose", 0, 1, 0, 0), ("apply_att", 1, -1)],
    (1, 1): [("project", 0, 0, -1), ("split_state", 0, 1, 0, 0)],
    (1, 2): [("transpose", 0, 1, 1, 0)],
    (1, 3): [("neighbours", 0, 1, 0, 0), ("project", 0, 1, -1)],
    (1, 4): [("split_state", 0, 1, 1, 0), ("project", 0, 2, -1)],
    (1, 5): [("neighbours", 0, 1, 1, 0), ("project", 0, 3, -1)],
    (1, 6): [("att_transpose", 1, 0, -1)],
    (1, 7): [("att_transpose", 1, 1, -1)],
    (2, 0): [("transpose", 1, 1, 0, 0), ("scores", 0, -1)],
    (2, 1): [("split_state", 1, 1, 0, 0), ("project", 1, 0, -1)],
    (2, 2): [("transpose", 1, 1, 1, 0), ("softmax", 0, -1)],
    (2, 3): [("neighbours", 1, 1, 0, 0), ("project", 1, 1, -1)],
    (2, 4): [("split_state", 1, 1, 1, 0), ("probs_transpose", 0, -1)],
    (2, 5): [("neighbours", 1, 1, 1, 0), ("project", 1, 2, -1)],
    (2, 6): [("project", 1, 3, -1)],
    (3, 0): [("transpose", 0, 2, 0, 0), ("scores", 1, -1)],
    (3, 1): [("split_state", 0, 2, 0, 0), ("attend", 0, 0, -1)],
    (3, 2): [("transpose", 0, 2, 1, 0), ("softmax", 1, -1)],
    (3, 3): [("neighbours", 0, 2, 0, 0), ("attend", 0, 1, -1)],
    (3, 4): [("split_state", 0, 2, 1, 0), ("probs_transpose", 1, -1)],
    (3, 5): [("neighbours", 0, 2, 1, 0)],
    (4, 0): [("transpose", 1, 2, 0, 0)],
    (4, 1): [("split_state", 1, 2, 0, 0), ("attend", 1, 0, -1)],
    (4, 2): [("transpose", 1, 2, 1, 0), ("stats_gnn", 0, 1)],
    (4, 3): [("neighbours", 1, 2, 0, 0), ("attend", 1, 1, -1)],
    (4, 4): [("split_state", 1, 2, 1, 0)],
    (4, 5): [("neighbours", 1, 2, 1, 0), ("apply_gnn", 0, 1)],
    (4, 7): [("split_gnn", 0, 1)],
    (5, 0): [("residual", 0, 0, 0)],
    (5, 1): [("first_transpose", 0, 0, 1)],
    (5, 2): [("residual", 0, 1, 0), ("stats_gnn", 1, 1)],
    (5, 3): [("first_transpose", 0, 1, 1)],
    (5, 4): [("neighbours", 0, 0, 0, 1), ("stats_att", 0, 0)],
    (5, 5): [("neighbours", 0, 0, 1, 1), ("apply_gnn", 1, 1)],
    (5, 6): [("split_gnn", 1, 1)],
    (5, 7): [("apply_att", 0, 0)],
}
PROLOGUE = [("stats_gnn", 0, 0), ("apply_gnn", 0, 0), ("split_gnn", 0, 0), ("first_transpose", 0, 0, 0),
            ("first_transpose", 0, 1, 0), ("stats_gnn", 1, 0), ("neighbours", 0, 0, 0, 0), ("neighbours", 0, 0, 1, 0),
            ("apply_gnn", 1, 0), ("split_gnn", 1, 0)]


def per_group(p, a):
    return p * 2 + a + 1


def per_chunk(p, a, c):
    return p * 4 + 2 * a + c + 1


def per_graph(p, a, b):
    return p * 8 + 4 * a + b + 1


def per_gate(p, a, layer, c):
    return p * 12 + 4 * layer + 2 * a + c + 1


def per_later_layer(p, a, layer, c):
    return p * 8 + 4 * (layer - 1) + 2 * a + c + 1


def per_load(p):
    return p * 16 + 16


def wait_reached(engine, semaphore, count):
    if not (isinstance(count, int) and count < 1):
        engine.wait_ge(semaphore, count)


def graph_blocks(nc, x, adj, weight, w_ih, w_hh, b_ih, b_hh, att_w, att_a, out):
    graphs = x.shape[0]
    pairs = graphs // (2 * GROUP)
    assert x.shape[1:] == (P, D) and weight.shape[0] == LAYERS and graphs == pairs * 2 * GROUP

    ctx = ExitStack()
    with ctx:
        def sb(name, shape, dtype):
            return ctx.enter_context(nc.sbuf_tensor(name, shape, dtype))

        def sem(name):
            return ctx.enter_context(nc.semaphore(name))

        ident = sb("ident", [P, P], F32)
        wi_hi = sb("wi_hi", [P, LAYERS, KC, 3 * D], F32R)
        wi_lo = sb("wi_lo", [P, LAYERS, KC, 3 * D], F32R)
        wh_hi = sb("wh_hi", [P, KC, 3 * D], F32R)
        wh_lo = sb("wh_lo", [P, KC, 3 * D], F32R)
        wa_hi = sb("wa_hi", [P, KC, D + 2], F32R)
        wa_lo = sb("wa_lo", [P, KC, D + 2], F32R)
        bih = sb("bih", [P, GATES], F32)
        bhh = sb("bhh", [P, GATES], F32)
        b_rz = sb("b_rz", [P, 4], F32)
        b_hn = sb("b_hn", [P, KC], F32)
        consts = sb("consts", [P, 4, GROUP], F32)
        quarter, per_d, eps, minus_half = (consts[:, i, :] for i in range(4))

        with ExitStack() as setup:
            def tmp(name, shape, dtype=F32):
                return setup.enter_context(nc.sbuf_tensor(name, shape, dtype))

            raw_ih = tmp("raw_ih", [P, GATES, D])
            raw_hh = tmp("raw_hh", [P, GATES, D])
            raw_w = tmp("raw_w", [P, LAYERS, KC, D])
            raw_att = tmp("raw_att", [P, KC, D])
            att_col = tmp("att_col", [P, 2, KC])
            ih_t = tmp("ih_t", [P, KC, 3 * D])
            w_t = tmp("w_t", [P, LAYERS, KC, D])
            banks = [setup.enter_context(nc.psum_tensor(f"setup_bank{i}", [P, 512], F32)) for i in range(4)]
            loaded = setup.enter_context(nc.semaphore("loaded"))
            ident_ready = setup.enter_context(nc.semaphore("ident_ready"))
            bank_full = setup.enter_context(nc.semaphore("bank_full"))
            hi_ready = setup.enter_context(nc.semaphore("hi_ready"))
            bank_read = setup.enter_context(nc.semaphore("bank_read"))
            bias_step = setup.enter_context(nc.semaphore("bias_step"))
            LOADS = 7

            fills = [("ih", k, half) for k in range(KC) for half in range(2)]
            fills += [("w", layer, k) for layer in range(LAYERS) for k in range(KC)]
            fills += [("hh", k, part) for k in range(KC) for part in range(2)]
            fills += [("att", k, 0) for k in range(KC)]
            plain = len([f for f in fills if f[0] in ("ih", "w")])
            fills += [("wi", (layer, k), part) for layer in range(LAYERS) for k in range(KC) for part in range(2)]
            COLS = (slice(0, 2 * D), slice(2 * D, 3 * D))
            HALF = (slice(0, 3 * P), slice(3 * P, 6 * P))

            with nc.Block() as block:
                @block.sync
                def _(sp):
                    sp.dma_start(raw_ih[:], w_ih.rearrange("(c p) e -> p c e", p=P)).then_inc(loaded, 16)
                    sp.dma_start(raw_w[:], weight.rearrange("l (c p) e -> p l c e", p=P)).then_inc(loaded, 16)
                    sp.dma_start(raw_hh[:], w_hh.rearrange("(c p) e -> p c e", p=P)).then_inc(loaded, 16)
                    sp.dma_start(raw_att[:], att_w.rearrange("(c p) f -> p c f", p=P)).then_inc(loaded, 16)
                    with nc.allow_non_contiguous_dma(reason="small vectors, once"):
                        sp.dma_start(att_col[:], att_a.rearrange("o (w k p) -> p (o w) k", w=2, p=P)).then_inc(loaded, 16)
                        sp.dma_start(bih[:], b_ih.rearrange("(c p) -> p c", p=P)).then_inc(loaded, 16)
                        sp.dma_start(bhh[:], b_hh.rearrange("(c p) -> p c", p=P)).then_inc(loaded, 16)

                @block.gpsimd
                def _(pool):
                    nc.gpsimd.memset(ident[:], 0.0).then_inc(ident_ready, 1)
                    nc.gpsimd.memset(quarter, 0.25)
                    nc.gpsimd.memset(per_d, 1.0 / D)
                    nc.gpsimd.memset(eps, EPS)
                    nc.gpsimd.memset(minus_half, -0.5)
                    pool.wait_ge(ident_ready, 1)
                    nc.gpsimd.affine_select(out=ident[:], in_=ident[:], compare_op=ALU.not_equal, fill=1.0, base=0,
                                            pattern=[[-1, P]], channel_multiplier=1).then_inc(ident_ready, 1)

                @block.tensor
                def _(pe):
                    pe.wait_ge(ident_ready, 2)
                    pe.wait_ge(loaded, 16 * LOADS)
                    for n, (what, where, which) in enumerate(fills):
                        bank = banks[n % 4]
                        if n >= 4:
                            pe.wait_ge(bank_read, n - 3)
                        if what == "ih":
                            for j in range(3):
                                last = nc.tensor.transpose(bank[:, j * P:(j + 1) * P],
                                                           raw_ih[:, 3 * which + j, where * P:(where + 1) * P], ident[:])
                        elif what == "w":
                            for j in range(KC):
                                last = nc.tensor.transpose(bank[:, j * P:(j + 1) * P],
                                                           raw_w[:, where, j, which * P:(which + 1) * P], ident[:])
                        elif what == "hh":
                            for j in range(4 if which == 0 else 2):
                                last = nc.tensor.transpose(bank[:, j * P:(j + 1) * P],
                                                           raw_hh[:, 4 * which + j, where * P:(where + 1) * P], ident[:])
                        elif what == "att":
                            for j in range(KC):
                                last = nc.tensor.transpose(bank[:, j * P:(j + 1) * P],
                                                           raw_att[:, j, where * P:(where + 1) * P], ident[:])
                            for j in range(KC):
                                last = nc.tensor.matmul(bank[:, D:D + 2], raw_att[:, j, where * P:(where + 1) * P],
                                                        att_col[:, :, j], start=(j == 0), stop=(j == KC - 1))
                        else:
                            layer, k = where
                            cols = COLS[which]
                            pe.wait_ge(bank_read, plain)
                            for e in range(KC):
                                last = nc.tensor.matmul(bank[:, 0:cols.stop - cols.start],
                                                        w_t[:, layer, e, k * P:(k + 1) * P], ih_t[:, e, cols],
                                                        start=(e == 0), stop=(e == KC - 1))
                        last.then_inc(bank_full, 1)

                def split_target(what, where, which):
                    if what == "hh":
                        return wh_hi[:, where, COLS[which]], wh_lo[:, where, COLS[which]], (0.5 if which else 1.0)
                    if what == "att":
                        return wa_hi[:, where, :], wa_lo[:, where, :], 1.0
                    layer, k = where
                    return wi_hi[:, layer, k, COLS[which]], wi_lo[:, layer, k, COLS[which]], 1.0

                @block.scalar
                def _(act):
                    for n, fill in enumerate(fills):
                        if fill[0] in ("ih", "w"):
                            continue
                        hi, _, scale = split_target(*fill)
                        act.wait_ge(bank_full, n + 1)
                        nc.scalar.activation(hi, banks[n % 4][:, 0:hi.shape[-1]], ACT.Copy,
                                             scale=scale).then_inc(hi_ready, 1)

                @block.vector
                def _(dve):
                    for n, (what, where, which) in enumerate(fills):
                        dve.wait_ge(bank_full, n + 1)
                        bank = banks[n % 4]
                        if what == "ih":
                            nc.vector.tensor_copy(ih_t[:, where, HALF[which]], bank[:, 0:3 * P]).then_inc(bank_read, 1)
                        elif what == "w":
                            nc.vector.tensor_copy(w_t[:, where, which, :], bank[:, 0:D]).then_inc(bank_read, 1)
                        else:
                            hi, lo, scale = split_target(what, where, which)
                            dve.wait_ge(hi_ready, n - plain + 1)
                            nc.vector.scalar_tensor_tensor(lo, bank[:, 0:lo.shape[-1]], scale, hi.bitcast(F32),
                                                           ALU.mult, ALU.subtract).then_inc(bank_read, 1)
                    nc.vector.tensor_tensor(b_rz[:], bih[:, 0:4], bhh[:, 0:4], ALU.add).then_inc(bias_step, 1)
                    dve.wait_ge(bias_step, 1)
                    nc.vector.tensor_scalar(b_rz[:], b_rz[:], 0.5, None, ALU.mult)
                    nc.vector.tensor_scalar(b_hn[:], bhh[:, 4:6], 0.5, None, ALU.mult)

        def both(name, shape, dtype):
            return [sb(f"{name}{a}", shape, dtype) for a in range(2)]

        x_in = both("x_in", [P, GROUP, D], F32)
        x_res = both("x_res", [P, GROUP, D], F32)
        adj_in = both("adj_in", [P, GROUP, P], I32)
        adj_att = both("adj_att", [P, GROUP, P], I32)
        adj_s = both("adj_s", [P, GROUP, P], F16)
        ht = both("ht", [P, KC, T], F32)
        ht_hi = [both(f"ht_hi{q}_", [P, KC, T], F32R) for q in range(2)]
        ht_lo = [both(f"ht_lo{q}_", [P, KC, T], F32R) for q in range(2)]
        h_hi = both("h_hi", [P, KC, GROUP, P], F16)
        h_lo = both("h_lo", [P, KC, GROUP, P], F16)
        nb_hi = both("nb_hi", [P, KC, T], F32R)
        nb_lo = both("nb_lo", [P, KC, T], F32R)
        wh_out_hi = both("wh_out_hi", [P, GROUP, D], F32R)
        wh_out_lo = both("wh_out_lo", [P, GROUP, D], F32R)
        s12 = both("s12", [P, GROUP, 2], F32)
        row_scale = both("row_scale", [P, GROUP], F32)
        relu_gnn = sb("relu_gnn", [P, GROUP, D], F32)
        relu_att = sb("relu_att", [P, GROUP, D], F32)
        ut_hi = sb("ut_hi", [P, KC, T], F32R)
        ut_lo = sb("ut_lo", [P, KC, T], F32R)
        hn_b = [sb(f"hn_b{c}", [P, T], F32) for c in range(2)]
        tanh_r = [sb(f"tanh_r{c}", [P, T], F32) for c in range(2)]
        tanh_z = [sb(f"tanh_z{c}", [P, T], F32) for c in range(2)]
        n_pre = [sb(f"n_pre{c}", [P, T], F32) for c in range(2)]
        n_out = [sb(f"n_out{c}", [P, T], F32) for c in range(2)]
        diff = [sb(f"diff{c}", [P, T], F32) for c in range(2)]
        score = sb("score", [P, GROUP, P], F32)
        prob = sb("prob", [P, GROUP, P], F32)
        pt_hi = sb("pt_hi", [P, GROUP, P], F32R)
        pt_lo = sb("pt_lo", [P, GROUP, P], F32R)
        row_max = sb("row_max", [P, GROUP], F32)
        minus_max = sb("minus_max", [P, GROUP], F32)
        row_sum = sb("row_sum", [P, GROUP], F32)
        row_inv = sb("row_inv", [P, GROUP], F32)
        KINDS = ("gnn", "att")
        stats = {k: sb(f"stats_{k}", [P, GROUP, 6], F32) for k in KINDS}
        ln_all = {k: sb(f"ln_{k}", [P, 11, GROUP], F32) for k in KINDS}
        ln = {k: [ln_all[k][:, i, :] for i in range(11)] for k in KINDS}

        def bank(name):
            return ctx.enter_context(nc.psum_tensor(name, [P, 512], F32))

        hn_bank, r_bank, in_bank, z_bank = bank("hn_bank"), bank("r_bank"), bank("in_bank"), bank("z_bank")
        nb_bank, t_bank, w_bank, s_bank = bank("nb_bank"), bank("t_bank"), bank("w_bank"), bank("s_bank")

        x_in_loaded = [sem(f"x_in_loaded{a}") for a in range(2)]
        adj_in_loaded = [sem(f"adj_in_loaded{a}") for a in range(2)]
        x_res_loaded = [sem(f"x_res_loaded{a}") for a in range(2)]
        adj_att_loaded = [sem(f"adj_att_loaded{a}") for a in range(2)]
        out_stored = [sem(f"out_stored{a}") for a in range(2)]
        hn_done, r_done, in_done, z_done = sem("hn_done"), sem("r_done"), sem("in_done"), sem("z_done")
        nb_done = sem("nb_done")
        first_t_done, t_done, res_t_done, att_t_done = (sem("first_t_done"), sem("t_done"), sem("res_t_done"),
                                                        sem("att_t_done"))
        wh_done, s2_done, probs_t_done, attend_done = (sem("wh_done"), sem("s2_done"), sem("probs_t_done"),
                                                       sem("attend_done"))
        hn_ready, tanh_r_ready, n_ready, tanh_z_ready = (sem("hn_ready"), sem("tanh_r_ready"), sem("n_ready"),
                                                         sem("tanh_z_ready"))
        ht_hi_ready, first_ht_hi_ready = sem("ht_hi_ready"), sem("first_ht_hi_ready")
        h_hi_ready, first_h_hi_ready = sem("h_hi_ready"), sem("first_h_hi_ready")
        nb_hi_ready = sem("nb_hi_ready")
        relu_gnn_ready, relu_att_ready = sem("relu_gnn_ready"), sem("relu_att_ready")
        ut_hi_ready, wh_hi_ready, prob_ready, pt_hi_ready = (sem("ut_hi_ready"), sem("wh_hi_ready"),
                                                             sem("prob_ready"), sem("pt_hi_ready"))
        rn_ready, n_pre_ready, diff_ready, zdiff_ready, h_ready = (sem("rn_ready"), sem("n_pre_ready"),
                                                                   sem("diff_ready"), sem("zdiff_ready"),
                                                                   sem("h_ready"))
        ht_lo_ready, first_ht_lo_ready = sem("ht_lo_ready"), sem("first_ht_lo_ready")
        h_lo_ready, first_h_lo_ready = sem("h_lo_ready"), sem("first_h_lo_ready")
        nb_lo_ready, adj_s_ready, x1_ready = sem("nb_lo_ready"), sem("adj_s_ready"), sem("x1_ready")
        stats_ready = {k: sem(f"stats_{k}_ready") for k in KINDS}
        ut_lo_ready, wh_lo_ready, pt_lo_ready = sem("ut_lo_ready"), sem("wh_lo_ready"), sem("pt_lo_ready")
        mask_ready, sum_ready, leaky_ready, masked_ready, max_ready, minus_max_ready = (
            sem("mask_ready"), sem("sum_ready"), sem("leaky_ready"), sem("masked_ready"), sem("max_ready"),
            sem("minus_max_ready"))
        inv_ready, row_scale_ready, out_ready = sem("inv_ready"), sem("row_scale_ready"), sem("out_ready")
        ln_step = {k: sem(f"ln_step_{k}") for k in KINDS}
        LN_STEPS = 10
        shift_ready = ln_step

        x_v = x.rearrange("(n b) t d -> n t b d", b=GROUP)
        out_v = out.rearrange("(n b) t d -> n t b d", b=GROUP)
        adj_v = adj.rearrange("(n b) s t -> n s b t", b=GROUP)

        def dram_group(view, index):
            return view[bass.ds(index, 1)].rearrange("n t b d -> (n t) b d")

        def exists(p):
            return not isinstance(p, int) or 0 <= p < pairs

        def slots(p, gate, side):
            for slot in range(2 * LAYERS):
                for step in range(len(STEPS)):
                    if exists(p):
                        gate(p, slot % 2, slot // 2, STEPS[step][:-1], step // 4)
                    for stage, *which, offset in SIDE.get((slot, step), ()):
                        if stage in side and exists(p + offset) and (exists(p) or offset < 0):
                            side[stage](p + offset, *which)

        def all_pairs(engine, gate, side):
            for stage, *which, _ in PROLOGUE:
                if stage in side:
                    side[stage](0, *which)
            slots(0, gate, side)
            with engine.Fori(1, pairs - 1) as p:
                slots(p, gate, side)
            slots(pairs - 1, gate, side)
            slots(pairs, gate, side)

        with nc.Block() as block:
            @block.sync
            def _(sp):
                def load_gnn(p, a):
                    index = sp.snap(p * 2 + a)
                    wait_reached(sp, relu_gnn_ready, per_group(p - 1, a))
                    sp.dma_start(x_in[a][:], dram_group(x_v, index)).then_inc(x_in_loaded[a], 16)
                    wait_reached(sp, adj_s_ready, per_group(p - 1, a))
                    sp.dma_start(adj_in[a][:], dram_group(adj_v, index)).then_inc(adj_in_loaded[a], 16)

                def store(p, a):
                    index = sp.snap(p * 2 + a)
                    sp.wait_ge(out_ready, per_chunk(p, a, 1))
                    sp.dma_start(dram_group(out_v, index), x_res[a][:]).then_inc(out_stored[a], 16)

                def load_att(p, a):
                    index = sp.snap(p * 2 + a)
                    wait_reached(sp, out_stored[a], per_load(p - 1))
                    sp.dma_start(x_res[a][:], dram_group(x_v, index)).then_inc(x_res_loaded[a], 16)
                    wait_reached(sp, mask_ready, per_group(p - 1, a))
                    sp.dma_start(adj_att[a][:], dram_group(adj_v, index)).then_inc(adj_att_loaded[a], 16)

                def pair(p):
                    for a in range(2):
                        if exists(p + 1):
                            load_gnn(p + 1, a)
                    for a in range(2):
                        if exists(p - 1):
                            store(p - 1, a)
                        load_att(p, a)

                load_gnn(0, 0)
                load_gnn(0, 1)
                pair(0)
                with sp.Fori(1, pairs - 1) as p:
                    pair(p)
                pair(pairs - 1)
                for a in range(2):
                    store(pairs - 1, a)
                for a in range(2):
                    sp.wait_ge(out_stored[a], per_load(pairs - 1))

            @block.tensor
            def _(pe):
                def products(bank_ap, terms):
                    todo = [m for w_hi, w_lo, d_hi, d_lo in terms for m in ((w_hi, d_hi), (w_hi, d_lo), (w_lo, d_hi))]
                    for i, (w, d) in enumerate(todo):
                        last = nc.tensor.matmul(bank_ap, w, d, start=(i == 0), stop=(i == len(todo) - 1))
                    return last

                def gate(p, a, layer, name, c):
                    n = per_gate(p, a, layer, c)
                    row = {"hn": 4, "r": 0, "in": 4, "z": 2}[name] + c
                    cols = slice(row * P, (row + 1) * P)
                    from_h = [(wh_hi[:, k, cols], wh_lo[:, k, cols], ht_hi[layer % 2][a][:, k, :],
                               ht_lo[layer % 2][a][:, k, :]) for k in range(KC)]
                    from_nb = [(wi_hi[:, layer, k, cols], wi_lo[:, layer, k, cols], nb_hi[a][:, k, :],
                                nb_lo[a][:, k, :]) for k in range(KC)]
                    if name == "hn":
                        if c == 0 and layer == 0:
                            pe.wait_ge(first_ht_lo_ready, per_chunk(p, a, 1))
                        elif c == 0:
                            pe.wait_ge(ht_lo_ready, per_later_layer(p, a, layer, 1))
                        wait_reached(pe, hn_ready, n - 1)
                        products(hn_bank[:], from_h).then_inc(hn_done, 1)
                    elif name == "r":
                        wait_reached(pe, tanh_r_ready, n - 1)
                        if c == 0:
                            pe.wait_ge(nb_lo_ready, per_gate(p, a, layer, 1))
                        products(r_bank[:], from_h + from_nb).then_inc(r_done, 1)
                    elif name == "in":
                        wait_reached(pe, n_pre_ready, n - 1)
                        products(in_bank[:], from_nb).then_inc(in_done, 1)
                    else:
                        wait_reached(pe, tanh_z_ready, n - 1)
                        products(z_bank[:], from_h + from_nb).then_inc(z_done, 1)

                def group_transposes(source, blocks):
                    for b in range(GROUP):
                        last = nc.tensor.transpose(t_bank[:, b * P:(b + 1) * P], blocks(source, b), ident[:])
                    return last

                def columns_of(source, b):
                    return source[:, b * P:(b + 1) * P]

                def first_transpose(p, a, c):
                    pe.wait_ge(relu_gnn_ready, per_group(p, a))
                    wait_reached(pe, first_ht_lo_ready, per_chunk(p, a, c) - 1)
                    wait_reached(pe, x1_ready, per_chunk(p - 1, a, c))
                    group_transposes(relu_gnn, lambda s, b: s[:, b, c * P:(c + 1) * P]).then_inc(first_t_done, 1)

                def transpose(p, a, layer, c):
                    pe.wait_ge(h_ready, per_gate(p, a, layer - 1, c))
                    wait_reached(pe, h_lo_ready, per_later_layer(p, a, layer, c) - 1)
                    if layer == 1 and a == 0 and c == 0:
                        pe.wait_ge(first_ht_lo_ready, per_chunk(p, 1, 1))
                    if layer == 1 and c == 0:
                        wait_reached(pe, ut_lo_ready, per_chunk(p - 1, a, 1))
                    group_transposes(ht[a][:, c, :], columns_of).then_inc(t_done, 1)

                def residual(p, a, c):
                    pe.wait_ge(h_ready, per_gate(p, a, LAYERS - 1, c))
                    wait_reached(pe, x1_ready, per_chunk(p, a, c) - 1)
                    if a == 0 and c == 0:
                        pe.wait_ge(h_lo_ready, per_later_layer(p, 1, 2, 1))
                    if exists(p + 1) and (a, c) != (0, 0):
                        before = (0, 0) if a == 0 else ((0, 1) if c == 0 else (1, 0))
                        pe.wait_ge(first_ht_lo_ready, per_chunk(p + 1, *before))
                    group_transposes(ht[a][:, c, :], columns_of).then_inc(res_t_done, 1)

                def att_transpose(p, a, c):
                    pe.wait_ge(relu_att_ready, per_group(p, a))
                    wait_reached(pe, ut_lo_ready, per_chunk(p, a, c) - 1)
                    if a == 0 and c == 0:
                        pe.wait_ge(x1_ready, per_chunk(p, 1, 1))
                        if exists(p + 1):
                            pe.wait_ge(first_ht_lo_ready, per_chunk(p + 1, 1, 1))
                    if a == 1 and c == 0 and exists(p + 1):
                        pe.wait_ge(h_lo_ready, per_later_layer(p + 1, 0, 1, 1))
                    group_transposes(relu_att, lambda s, b: s[:, b, c * P:(c + 1) * P]).then_inc(att_t_done, 1)

                def neighbours(p, a, layer, c):
                    n = per_gate(p, a, layer, c)
                    if layer == 0:
                        pe.wait_ge(first_h_lo_ready, per_group(p, a))
                        pe.wait_ge(adj_s_ready, per_group(p, a))
                    else:
                        pe.wait_ge(h_lo_ready, per_later_layer(p, a, layer, c))
                    wait_reached(pe, nb_lo_ready, n - 1)
                    for b in range(GROUP):
                        block_ap = nb_bank[:, b * P:(b + 1) * P]
                        nc.tensor.matmul(block_ap, h_hi[a][:, c, b, :], adj_s[a][:, b, :], start=True, stop=False)
                        last = nc.tensor.matmul(block_ap, h_lo[a][:, c, b, :], adj_s[a][:, b, :],
                                                start=False, stop=True)
                    last.then_inc(nb_done, 1)

                def project(p, a, b):
                    pe.wait_ge(ut_lo_ready, per_chunk(p, a, 1))
                    wait_reached(pe, wh_lo_ready, per_graph(p, a, b) - 1)
                    if a == 0 and b == 0:
                        wait_reached(pe, out_ready, per_chunk(p - 1, 1, 1))
                    nodes = slice(b * P, (b + 1) * P)
                    products(w_bank[:, 0:D + 2],
                             [(ut_hi[:, k, nodes], ut_lo[:, k, nodes], wa_hi[:, k, :], wa_lo[:, k, :])
                              for k in range(KC)]).then_inc(wh_done, 1)

                def scores(p, a):
                    pe.wait_ge(wh_lo_ready, per_graph(p, a, GROUP - 1))
                    wait_reached(pe, pt_lo_ready, per_group(p, a) - 1)
                    for b in range(GROUP):
                        last = nc.tensor.transpose(s_bank[:, b * P:(b + 1) * P],
                                                   s12[a][:, b, 1:2].broadcast_to([P, P]), ident[:])
                    last.then_inc(s2_done, 1)

                def probs_transpose(p, a):
                    pe.wait_ge(prob_ready, per_group(p, a))
                    for b in range(GROUP):
                        last = nc.tensor.transpose(s_bank[:, b * P:(b + 1) * P], prob[:, b, :], ident[:])
                    last.then_inc(probs_t_done, 1)

                def attend(p, a, half):
                    pe.wait_ge(pt_lo_ready, per_group(p, a))
                    wait_reached(pe, out_ready, per_chunk(p, a, half) - 1)
                    if a == 0 and half == 0:
                        pe.wait_ge(wh_lo_ready, per_graph(p, 1, GROUP - 1))
                    for i in range(2):
                        b = 2 * half + i
                        last = products(w_bank[:, i * D:(i + 1) * D],
                                        [(pt_hi[:, b, :], pt_lo[:, b, :], wh_out_hi[a][:, b, :], wh_out_lo[a][:, b, :])])
                    last.then_inc(attend_done, 1)

                all_pairs(pe, gate, {
                    "first_transpose": first_transpose, "transpose": transpose, "residual": residual,
                    "att_transpose": att_transpose, "neighbours": neighbours, "project": project, "scores": scores,
                    "probs_transpose": probs_transpose, "attend": attend})

            @block.scalar
            def _(act):
                def gate(p, a, layer, name, c):
                    n = per_gate(p, a, layer, c)
                    if name == "hn":
                        act.wait_ge(hn_done, n)
                        wait_reached(act, rn_ready, n - 2)
                        nc.scalar.activation(hn_b[c][:], hn_bank[:], ACT.Identity,
                                             bias=b_hn[:, c:c + 1]).then_inc(hn_ready, 1)
                    elif name == "r":
                        act.wait_ge(r_done, n)
                        wait_reached(act, rn_ready, n - 2)
                        nc.scalar.activation(tanh_r[c][:], r_bank[:], ACT.Tanh, bias=b_rz[:, c:c + 1],
                                             scale=0.5).then_inc(tanh_r_ready, 1)
                    elif name == "in":
                        act.wait_ge(n_pre_ready, n)
                        wait_reached(act, h_ready, n - 2)
                        nc.scalar.activation(n_out[c][:], n_pre[c][:], ACT.Tanh,
                                             bias=bih[:, 4 + c:5 + c]).then_inc(n_ready, 1)
                    else:
                        act.wait_ge(z_done, n)
                        wait_reached(act, zdiff_ready, n - 2)
                        nc.scalar.activation(tanh_z[c][:], z_bank[:], ACT.Tanh, bias=b_rz[:, 2 + c:3 + c],
                                             scale=0.5).then_inc(tanh_z_ready, 1)

                def split_state(p, a, layer, c):
                    act.wait_ge(h_ready, per_gate(p, a, layer - 1, c))
                    nc.scalar.activation(ht_hi[layer % 2][a][:, c, :], ht[a][:, c, :],
                                         ACT.Copy).then_inc(ht_hi_ready, 1)

                def norm(kind, source, target, ready):
                    rstd, shift = ln[kind][7], ln[kind][9]
                    for b in range(GROUP):
                        last = nc.scalar.activation(target[:, b, :], source[:, b, :], ACT.Relu,
                                                    bias=shift[:, b:b + 1], scale=rstd[:, b:b + 1])
                    last.then_inc(ready, 1)

                def apply_gnn(p, a):
                    wait_reached(act, first_t_done, per_chunk(p, a, 0) - 1)
                    wait_reached(act, first_h_lo_ready, per_group(p, a) - 1)
                    act.wait_ge(ln_step["gnn"], per_group(p, a) * LN_STEPS)
                    norm("gnn", x_in[a], relu_gnn, relu_gnn_ready)
                    wait_reached(act, nb_done, per_gate(p - 1, a, 2, 1))
                    act.wait_ge(relu_gnn_ready, per_group(p, a))
                    for c in range(KC):
                        last = nc.scalar.activation(h_hi[a][:, c], relu_gnn[:, :, c * P:(c + 1) * P], ACT.Copy,
                                                    scale=HSCALE)
                    last.then_inc(first_h_hi_ready, 1)

                def apply_att(p, a):
                    wait_reached(act, att_t_done, per_chunk(p, a, 0) - 1)
                    act.wait_ge(ln_step["att"], per_group(p, a) * LN_STEPS)
                    norm("att", x_res[a], relu_att, relu_att_ready)

                def first_transpose(p, a, c):
                    act.wait_ge(first_t_done, per_chunk(p, a, c))
                    nc.scalar.activation(ht[a][:, c, :], t_bank[:], ACT.Copy)
                    nc.scalar.activation(ht_hi[0][a][:, c, :], t_bank[:], ACT.Copy).then_inc(first_ht_hi_ready, 1)

                def transpose(p, a, layer, c):
                    act.wait_ge(t_done, per_later_layer(p, a, layer, c))
                    nc.scalar.activation(h_hi[a][:, c].rearrange("p b t -> p (b t)"), t_bank[:], ACT.Copy,
                                         scale=HSCALE).then_inc(h_hi_ready, 1)

                def neighbours(p, a, layer, c):
                    act.wait_ge(nb_done, per_gate(p, a, layer, c))
                    nc.scalar.activation(nb_hi[a][:, c, :], nb_bank[:], ACT.Copy).then_inc(nb_hi_ready, 1)

                def att_transpose(p, a, c):
                    act.wait_ge(att_t_done, per_chunk(p, a, c))
                    wait_reached(act, wh_done, per_graph(p, a, 0) - 1)
                    nc.scalar.activation(ut_hi[:, c, :], t_bank[:], ACT.Copy).then_inc(ut_hi_ready, 1)

                def project(p, a, b):
                    act.wait_ge(wh_done, per_graph(p, a, b))
                    nc.scalar.activation(wh_out_hi[a][:, b, :], w_bank[:, 0:D], ACT.Copy).then_inc(wh_hi_ready, 1)

                def softmax(p, a):
                    act.wait_ge(minus_max_ready, per_group(p, a))
                    wait_reached(act, probs_t_done, per_group(p, a) - 1)
                    for b in range(GROUP):
                        last = nc.scalar.activation(prob[:, b, :], score[:, b, :], ACT.Exp,
                                                    bias=minus_max[:, b:b + 1], accum_out=row_sum[:, b:b + 1])
                    last.then_inc(prob_ready, 1)

                def probs_transpose(p, a):
                    act.wait_ge(probs_t_done, per_group(p, a))
                    nc.scalar.activation(pt_hi[:].rearrange("p b t -> p (b t)"), s_bank[:],
                                         ACT.Copy).then_inc(pt_hi_ready, 1)

                all_pairs(act, gate, {
                    "apply_gnn": apply_gnn, "apply_att": apply_att, "split_state": split_state,
                    "first_transpose": first_transpose, "transpose": transpose, "att_transpose": att_transpose,
                    "neighbours": neighbours, "project": project, "softmax": softmax,
                    "probs_transpose": probs_transpose})

            @block.vector
            def _(dve):
                def low_part(lo, whole, hi, ready):
                    nc.vector.tensor_tensor(lo, whole, hi.bitcast(F32), ALU.subtract).then_inc(ready, 1)

                def gate(p, a, layer, name, c):
                    n = per_gate(p, a, layer, c)
                    if name == "r":
                        dve.wait_ge(hn_ready, n)
                        dve.wait_ge(tanh_r_ready, n)
                        wait_reached(dve, n_ready, n - 2)
                        nc.vector.scalar_tensor_tensor(n_pre[c][:], tanh_r[c][:], 1.0, hn_b[c][:], ALU.add,
                                                       ALU.mult).then_inc(rn_ready, 1)
                    elif name == "in":
                        dve.wait_ge(rn_ready, n)
                        dve.wait_ge(in_done, n)
                        nc.vector.tensor_tensor(n_pre[c][:], n_pre[c][:], in_bank[:], ALU.add).then_inc(n_pre_ready, 1)
                    elif name == "z":
                        dve.wait_ge(n_ready, n)
                        wait_reached(dve, h_ready, n - 2)
                        nc.vector.tensor_tensor(diff[c][:], ht[a][:, c, :], n_out[c][:],
                                                ALU.subtract).then_inc(diff_ready, 1)
                        dve.wait_ge(diff_ready, n)
                        dve.wait_ge(tanh_z_ready, n)
                        nc.vector.scalar_tensor_tensor(diff[c][:], tanh_z[c][:], 1.0, diff[c][:], ALU.add,
                                                       ALU.mult).then_inc(zdiff_ready, 1)
                        dve.wait_ge(zdiff_ready, n)
                        nc.vector.scalar_tensor_tensor(ht[a][:, c, :], diff[c][:], 0.5, n_out[c][:], ALU.mult,
                                                       ALU.add).then_inc(h_ready, 1)

                def split_state(p, a, layer, c):
                    q = layer % 2
                    dve.wait_ge(ht_hi_ready, per_later_layer(p, a, layer, c))
                    low_part(ht_lo[q][a][:, c, :], ht[a][:, c, :], ht_hi[q][a][:, c, :], ht_lo_ready)

                def statistics(kind, source):
                    for b in range(GROUP):
                        last = nc.vector.bn_stats(stats[kind][:, b, :], source[:, b, :])
                    last.then_inc(stats_ready[kind], 1)

                def stats_gnn(p, a):
                    dve.wait_ge(x_in_loaded[a], per_load(p))
                    wait_reached(dve, ln_step["gnn"], (per_group(p, a) - 1) * LN_STEPS)
                    statistics("gnn", x_in[a])
                    dve.wait_ge(adj_in_loaded[a], per_load(p))
                    wait_reached(dve, nb_done, per_gate(p - 1, a, 2, 1))
                    nc.vector.tensor_scalar(adj_s[a][:], adj_in[a][:], 0.0, 1.0 / HSCALE, ALU.not_equal,
                                            ALU.mult).then_inc(adj_s_ready, 1)

                def split_gnn(p, a):
                    dve.wait_ge(first_h_hi_ready, per_group(p, a))
                    for c in range(KC):
                        last = nc.vector.scalar_tensor_tensor(h_lo[a][:, c], relu_gnn[:, :, c * P:(c + 1) * P], HSCALE,
                                                              h_hi[a][:, c], ALU.mult, ALU.subtract)
                    last.then_inc(first_h_lo_ready, 1)

                def stats_att(p, a):
                    dve.wait_ge(x1_ready, per_chunk(p, a, 1))
                    wait_reached(dve, ln_step["att"], (per_group(p, a) - 1) * LN_STEPS)
                    statistics("att", x_res[a])

                def first_transpose(p, a, c):
                    dve.wait_ge(first_ht_hi_ready, per_chunk(p, a, c))
                    low_part(ht_lo[0][a][:, c, :], t_bank[:], ht_hi[0][a][:, c, :], first_ht_lo_ready)

                def transpose(p, a, layer, c):
                    dve.wait_ge(h_hi_ready, per_later_layer(p, a, layer, c))
                    nc.vector.scalar_tensor_tensor(h_lo[a][:, c].rearrange("p b t -> p (b t)"), t_bank[:], HSCALE,
                                                   h_hi[a][:, c].rearrange("p b t -> p (b t)"), ALU.mult,
                                                   ALU.subtract).then_inc(h_lo_ready, 1)

                def residual(p, a, c):
                    dve.wait_ge(x_res_loaded[a], per_load(p))
                    dve.wait_ge(res_t_done, per_chunk(p, a, c))
                    part = x_res[a][:, :, c * P:(c + 1) * P]
                    nc.vector.tensor_tensor(part, part, t_bank[:].rearrange("p (b t) -> p b t", b=GROUP),
                                            ALU.add).then_inc(x1_ready, 1)

                def neighbours(p, a, layer, c):
                    dve.wait_ge(nb_hi_ready, per_gate(p, a, layer, c))
                    low_part(nb_lo[a][:, c, :], nb_bank[:], nb_hi[a][:, c, :], nb_lo_ready)

                def att_transpose(p, a, c):
                    dve.wait_ge(ut_hi_ready, per_chunk(p, a, c))
                    low_part(ut_lo[:, c, :], t_bank[:], ut_hi[:, c, :], ut_lo_ready)

                def project(p, a, b):
                    dve.wait_ge(wh_hi_ready, per_graph(p, a, b))
                    nc.vector.tensor_copy(s12[a][:, b, :], w_bank[:, D:D + 2])
                    low_part(wh_out_lo[a][:, b, :], w_bank[:, 0:D], wh_out_hi[a][:, b, :], wh_lo_ready)

                def scores(p, a):
                    n = per_group(p, a)
                    dve.wait_ge(adj_att_loaded[a], per_load(p))
                    wait_reached(dve, probs_t_done, n - 1)
                    nc.vector.tensor_scalar(prob[:], adj_att[a][:], 0.0, MASKED, ALU.is_equal,
                                            ALU.mult).then_inc(mask_ready, 1)
                    dve.wait_ge(s2_done, n)
                    wait_reached(dve, prob_ready, n - 1)
                    nc.vector.tensor_tensor(score[:], s_bank[:].rearrange("p (b t) -> p b t", b=GROUP),
                                            s12[a][:, :, 0:1].broadcast_to([P, GROUP, P]),
                                            ALU.add).then_inc(sum_ready, 1)
                    dve.wait_ge(sum_ready, n)
                    nc.vector.scalar_tensor_tensor(score[:], score[:], ALPHA, score[:], ALU.mult,
                                                   ALU.max).then_inc(leaky_ready, 1)
                    dve.wait_ge(leaky_ready, n)
                    dve.wait_ge(mask_ready, n)
                    nc.vector.tensor_tensor(score[:], score[:], prob[:], ALU.add).then_inc(masked_ready, 1)
                    dve.wait_ge(masked_ready, n)
                    nc.vector.tensor_reduce(row_max[:], score[:], AX_X, ALU.max).then_inc(max_ready, 1)
                    dve.wait_ge(max_ready, n)
                    nc.vector.tensor_scalar(minus_max[:], row_max[:], -1.0, None, ALU.mult).then_inc(minus_max_ready, 1)

                def probs_transpose(p, a):
                    n = per_group(p, a)
                    dve.wait_ge(prob_ready, n)
                    nc.vector.reciprocal(row_inv[:], row_sum[:]).then_inc(inv_ready, 1)
                    dve.wait_ge(inv_ready, n)
                    nc.vector.scalar_tensor_tensor(row_scale[a][:], row_max[:], 0.5 * MASKED, row_inv[:], ALU.is_gt,
                                                   ALU.mult).then_inc(row_scale_ready, 1)
                    dve.wait_ge(pt_hi_ready, n)
                    low_part(pt_lo[:].rearrange("p b t -> p (b t)"), s_bank[:],
                             pt_hi[:].rearrange("p b t -> p (b t)"), pt_lo_ready)

                def attend(p, a, half):
                    dve.wait_ge(attend_done, per_chunk(p, a, half))
                    dve.wait_ge(row_scale_ready, per_group(p, a))
                    for i in range(2):
                        b = 2 * half + i
                        last = nc.vector.scalar_tensor_tensor(x_res[a][:, b, :], w_bank[:, i * D:(i + 1) * D],
                                                              row_scale[a][:, b:b + 1], x_res[a][:, b, :], ALU.mult,
                                                              ALU.add)
                    last.then_inc(out_ready, 1)

                all_pairs(dve, gate, {
                    "stats_gnn": stats_gnn, "split_gnn": split_gnn, "stats_att": stats_att,
                    "split_state": split_state, "first_transpose": first_transpose,
                    "transpose": transpose, "residual": residual, "att_transpose": att_transpose,
                    "neighbours": neighbours, "project": project, "scores": scores,
                    "probs_transpose": probs_transpose, "attend": attend})

            @block.gpsimd
            def _(pool):
                def norm(kind, p, a, last_read, last_count):
                    base = (per_group(p, a) - 1) * LN_STEPS
                    st = stats[kind]
                    total, gap, m2, gap2, gap2_4, m2_d, var, rstd, scaled, shift, var_eps = ln[kind]
                    step = ln_step[kind]
                    pool.wait_ge(stats_ready[kind], per_group(p, a))
                    wait_reached(pool, last_read, last_count)
                    nc.gpsimd.tensor_tensor(total, st[:, :, 1], st[:, :, 4], ALU.add).then_inc(step, 1)
                    nc.gpsimd.tensor_tensor(gap, st[:, :, 1], st[:, :, 4], ALU.subtract).then_inc(step, 1)
                    nc.gpsimd.tensor_tensor(m2, st[:, :, 2], st[:, :, 5], ALU.add).then_inc(step, 1)
                    pool.wait_ge(step, base + 2)
                    nc.gpsimd.tensor_tensor(scaled, total, minus_half, ALU.mult)
                    nc.gpsimd.tensor_tensor(gap2, gap, gap, ALU.mult).then_inc(step, 1)
                    pool.wait_ge(step, base + 3)
                    nc.gpsimd.tensor_tensor(m2_d, m2, per_d, ALU.mult).then_inc(step, 1)
                    pool.wait_ge(step, base + 4)
                    nc.gpsimd.tensor_tensor(gap2_4, gap2, quarter, ALU.mult).then_inc(step, 1)
                    pool.wait_ge(step, base + 6)
                    nc.gpsimd.tensor_tensor(var, gap2_4, m2_d, ALU.add).then_inc(step, 1)
                    pool.wait_ge(step, base + 7)
                    nc.gpsimd.tensor_tensor(var_eps, var, eps, ALU.add).then_inc(step, 1)
                    pool.wait_ge(step, base + 8)
                    nc.gpsimd.tensor_tensor(rstd, var_eps, minus_half, ALU.pow).then_inc(step, 1)
                    pool.wait_ge(step, base + 9)
                    nc.gpsimd.tensor_tensor(shift, scaled, rstd, ALU.mult).then_inc(step, 1)

                def stats_gnn(p, a):
                    norm("gnn", p, a, relu_gnn_ready, per_group(p, a) - 1)

                def stats_att(p, a):
                    norm("att", p, a, relu_att_ready, per_group(p, a) - 1)

                all_pairs(pool, lambda *step: None, {"stats_gnn": stats_gnn, "stats_att": stats_att})


_INS = ["x", "adj", "L0_gnn_weight", "L0_gnn_w_ih", "L0_gnn_w_hh", "L0_gnn_b_ih", "L0_gnn_b_hh", "L1_gnn_W",
        "L1_gnn_a"]


def kernel(**inputs):
    import numpy as _np
    import concourse.bacc as _bacc
    from concourse import mybir as _mybir
    from concourse.bass_utils import run_bass_kernel_spmd as _run

    nc = _bacc.Bacc("TRN2", target_bir_lowering=False, num_devices=1)
    arrays, args = {}, []
    for name in _INS:
        a = _np.ascontiguousarray(inputs[name])
        arrays[f"in_{name}_dram"] = a
        args.append(nc.dram_tensor(f"in_{name}_dram", a.shape, _mybir.dt.from_np(a.dtype), kind="ExternalInput").ap())
    out = nc.dram_tensor("out_dram", inputs["x"].shape, _mybir.dt.float32, kind="ExternalOutput").ap()
    graph_blocks(nc, *args, out)
    r = _run(nc, [arrays], core_ids=[0])
    return r.results[0]["out_dram"]
```

```python
from contextlib import ExitStack

import concourse.bass as bass
from concourse import mybir

F32 = mybir.dt.float32
F32R = mybir.dt.float32r
F16 = mybir.dt.float16
I32 = mybir.dt.int32
ALU = mybir.AluOpType
ACT = mybir.ActivationFunctionType
AX_X = mybir.AxisListType.X

P = 128
D = 256
KC = D // P
GROUP = 4
T = GROUP * P
LAYERS = 3
GATES = 3 * KC
ALPHA = 0.2
EPS = 1e-5
MASKED = -1e30
HSCALE = 2048.0

STEPS = ("hn0", "r0", "in0", "z0", "hn1", "r1", "in1", "z1")
SIDE = {
    (0, 0): [("residual", 1, 0, -1), ("update", 1, 2, 1, -1)],
    (0, 1): [("first_transpose", 1, 0, 0)],
    (0, 2): [("neighbours", 1, 0, 0, 0)],
    (0, 3): [("residual", 1, 1, -1)],
    (0, 4): [("first_transpose", 1, 1, 0), ("update", 0, 0, 0, 0)],
    (0, 5): [("neighbours", 1, 0, 1, 0)],
    (0, 6): [("att_transpose", 0, 0, -1), ("stats_att", 1, -1)],
    (0, 7): [("att_transpose", 0, 1, -1)],
    (1, 0): [("update", 0, 0, 1, 0), ("apply_att", 1, -1)],
    (1, 1): [("transpose", 0, 1, 0, 0), ("project", 0, 0, -1)],
    (1, 2): [("split_state", 0, 1, 0, 0)],
    (1, 3): [("transpose", 0, 1, 1, 0), ("project", 0, 1, -1)],
    (1, 4): [("update", 1, 0, 0, 0), ("neighbours", 0, 1, 0, 0)],
    (1, 5): [("split_state", 0, 1, 1, 0), ("project", 0, 2, -1)],
    (1, 6): [("neighbours", 0, 1, 1, 0)],
    (1, 7): [("project", 0, 3, -1)],
    (2, 0): [("update", 1, 0, 1, 0), ("att_transpose", 1, 0, -1)],
    (2, 1): [("transpose", 1, 1, 0, 0), ("scores", 0, -1)],
    (2, 2): [("split_state", 1, 1, 0, 0)],
    (2, 3): [("att_transpose", 1, 1, -1), ("softmax", 0, -1)],
    (2, 4): [("update", 0, 1, 0, 0), ("split_state", 1, 1, 1, 0), ("neighbours", 1, 1, 0, 0)],
    (2, 5): [("transpose", 1, 1, 1, 0), ("project", 1, 0, -1)],
    (2, 6): [("probs_transpose", 0, -1)],
    (2, 7): [("neighbours", 1, 1, 1, 0)],
    (3, 0): [("update", 0, 1, 1, 0)],
    (3, 1): [("transpose", 0, 2, 0, 0), ("project", 1, 1, -1)],
    (3, 2): [("split_state", 0, 2, 0, 0)],
    (3, 3): [("transpose", 0, 2, 1, 0), ("project", 1, 2, -1)],
    (3, 4): [("update", 1, 1, 0, 0), ("neighbours", 0, 2, 0, 0)],
    (3, 5): [("split_state", 0, 2, 1, 0), ("project", 1, 3, -1)],
    (3, 6): [("neighbours", 0, 2, 1, 0)],
    (3, 7): [("attend", 0, 0, -1)],
    (4, 0): [("update", 1, 1, 1, 0), ("scores", 1, -1)],
    (4, 1): [("transpose", 1, 2, 0, 0), ("attend", 0, 1, -1)],
    (4, 2): [("split_state", 1, 2, 0, 0), ("softmax", 1, -1)],
    (4, 3): [("transpose", 1, 2, 1, 0), ("stats_gnn", 0, 1)],
    (4, 4): [("update", 0, 2, 0, 0), ("neighbours", 1, 2, 0, 0)],
    (4, 5): [("probs_transpose", 1, -1), ("split_state", 1, 2, 1, 0), ("apply_gnn", 0, 1)],
    (4, 6): [("neighbours", 1, 2, 1, 0), ("split_gnn", 0, 1)],
    (4, 7): [("attend", 1, 0, -1)],
    (5, 0): [("residual", 0, 0, 0), ("update", 0, 2, 1, 0)],
    (5, 1): [("first_transpose", 0, 0, 1), ("attend", 1, 1, -1)],
    (5, 2): [("neighbours", 0, 0, 0, 1), ("stats_gnn", 1, 1)],
    (5, 3): [("residual", 0, 1, 0)],
    (5, 4): [("first_transpose", 0, 1, 1), ("update", 1, 2, 0, 0)],
    (5, 5): [("neighbours", 0, 0, 1, 1), ("stats_att", 0, 0)],
    (5, 6): [("apply_gnn", 1, 1)],
    (5, 7): [("split_gnn", 1, 1), ("apply_att", 0, 0)],
}
HEAD = [("first_transpose", 0, 0), ("neighbours", 0, 0, 0), ("stats_gnn", 1), ("first_transpose", 0, 1),
        ("neighbours", 0, 0, 1), ("apply_gnn", 1), ("split_gnn", 1)]
TAIL = [("residual", 1, 0), ("update", 1, 2, 1), ("residual", 1, 1), ("att_transpose", 0, 0), ("stats_att", 1),
        ("att_transpose", 0, 1), ("project", 0, 0), ("project", 0, 1), ("project", 0, 2), ("project", 0, 3),
        ("apply_att", 1), ("scores", 0), ("att_transpose", 1, 0), ("att_transpose", 1, 1), ("softmax", 0),
        ("project", 1, 0), ("project", 1, 1), ("project", 1, 2), ("project", 1, 3),
        ("probs_transpose", 0), ("scores", 1), ("softmax", 1), ("attend", 0, 0), ("attend", 0, 1), ("probs_transpose", 1),
        ("attend", 1, 0), ("attend", 1, 1)]


def per_group(p, a):
    return p * 2 + a + 1


def per_chunk(p, a, c):
    return p * 4 + 2 * a + c + 1


def per_graph(p, a, b):
    return p * 8 + 4 * a + b + 1


def per_gate(p, a, layer, c):
    return p * 12 + 4 * layer + 2 * a + c + 1


def per_later_layer(p, a, layer, c):
    return p * 8 + 4 * (layer - 1) + 2 * a + c + 1


def per_load(p):
    return p * 16 + 16


def wait_reached(engine, semaphore, count):
    if not (isinstance(count, int) and count < 1):
        engine.wait_ge(semaphore, count)


def graph_blocks(nc, x, adj, weight, w_ih, w_hh, b_ih, b_hh, att_w, att_a, out):
    graphs = x.shape[0]
    pairs = graphs // (2 * GROUP)
    assert x.shape[1:] == (P, D) and weight.shape[0] == LAYERS and graphs == pairs * 2 * GROUP

    ctx = ExitStack()
    with ctx:
        def sb(name, shape, dtype):
            return ctx.enter_context(nc.sbuf_tensor(name, shape, dtype))

        def sem(name):
            return ctx.enter_context(nc.semaphore(name))

        ident = sb("ident", [P, P], F32)
        wi_hi = sb("wi_hi", [P, LAYERS, KC, 3 * D], F32R)
        wi_lo = sb("wi_lo", [P, LAYERS, KC, 3 * D], F32R)
        wh_hi = sb("wh_hi", [P, KC, 3 * D], F32R)
        wh_lo = sb("wh_lo", [P, KC, 3 * D], F32R)
        wa_hi = sb("wa_hi", [P, KC, D + 2], F32R)
        wa_lo = sb("wa_lo", [P, KC, D + 2], F32R)
        bih = sb("bih", [P, GATES], F32)
        bhh = sb("bhh", [P, GATES], F32)
        b_rz = sb("b_rz", [P, 4], F32)
        b_hn = sb("b_hn", [P, KC], F32)
        consts = sb("consts", [P, 4, GROUP], F32)
        quarter, per_d, eps, minus_half = (consts[:, i, :] for i in range(4))

        def both(name, shape, dtype):
            return [sb(f"{name}{a}", shape, dtype) for a in range(2)]

        x_in = both("x_in", [P, GROUP, D], F32)
        adj_in = both("adj_in", [P, GROUP, P], I32)
        adj_s = both("adj_s", [P, GROUP, P], F16)
        h_hi = both("h_hi", [P, KC, GROUP, P], F16)
        h_lo = both("h_lo", [P, KC, GROUP, P], F16)
        relu_gnn = sb("relu_gnn", [P, GROUP, D], F32)
        KINDS = ("gnn", "att")
        stats = {k: sb(f"stats_{k}", [P, GROUP, 6], F32) for k in KINDS}
        ln_all = {k: sb(f"ln_{k}", [P, 11, GROUP], F32) for k in KINDS}
        ln = {k: [ln_all[k][:, i, :] for i in range(11)] for k in KINDS}
        x_in_loaded = [sem(f"x_in_loaded{a}") for a in range(2)]
        adj_in_loaded = [sem(f"adj_in_loaded{a}") for a in range(2)]
        relu_gnn_ready, first_h_hi_ready = sem("relu_gnn_ready"), sem("first_h_hi_ready")
        adj_s_ready, first_h_lo_ready = sem("adj_s_ready"), sem("first_h_lo_ready")
        stats_ready = {k: sem(f"stats_{k}_ready") for k in KINDS}
        ln_step = {k: sem(f"ln_step_{k}") for k in KINDS}
        LN_STEPS = 10
        nb_done, first_t_done = sem("nb_done"), sem("first_t_done")

        x_v = x.rearrange("(n b) t d -> n t b d", b=GROUP)
        out_v = out.rearrange("(n b) t d -> n t b d", b=GROUP)
        adj_v = adj.rearrange("(n b) s t -> n s b t", b=GROUP)

        def dram_group(view, index):
            return view[bass.ds(index, 1)].rearrange("n t b d -> (n t) b d")

        def exists(p):
            return not isinstance(p, int) or 0 <= p < pairs

        def load_gnn(sp, p, a):
            index = sp.snap(p * 2 + a)
            wait_reached(sp, relu_gnn_ready, per_group(p - 1, a))
            sp.dma_start(x_in[a][:], dram_group(x_v, index)).then_inc(x_in_loaded[a], 16)
            wait_reached(sp, adj_s_ready, per_group(p - 1, a))
            sp.dma_start(adj_in[a][:], dram_group(adj_v, index)).then_inc(adj_in_loaded[a], 16)

        def statistics(kind, source):
            for b in range(GROUP):
                last = nc.vector.bn_stats(stats[kind][:, b, :], source[:, b, :])
            last.then_inc(stats_ready[kind], 1)

        def stats_gnn(dve, p, a):
            dve.wait_ge(x_in_loaded[a], per_load(p))
            wait_reached(dve, ln_step["gnn"], (per_group(p, a) - 1) * LN_STEPS)
            statistics("gnn", x_in[a])
            dve.wait_ge(adj_in_loaded[a], per_load(p))
            wait_reached(dve, nb_done, per_gate(p - 1, a, 2, 1))
            nc.vector.tensor_scalar(adj_s[a][:], adj_in[a][:], 0.0, 1.0 / HSCALE, ALU.not_equal,
                                    ALU.mult).then_inc(adj_s_ready, 1)

        def split_gnn(dve, p, a):
            dve.wait_ge(first_h_hi_ready, per_group(p, a))
            for c in range(KC):
                last = nc.vector.scalar_tensor_tensor(h_lo[a][:, c], relu_gnn[:, :, c * P:(c + 1) * P], HSCALE,
                                                      h_hi[a][:, c], ALU.mult, ALU.subtract)
            last.then_inc(first_h_lo_ready, 1)

        def norm(kind, source, target, ready):
            rstd, shift = ln[kind][7], ln[kind][9]
            for b in range(GROUP):
                last = nc.scalar.activation(target[:, b, :], source[:, b, :], ACT.Relu,
                                            bias=shift[:, b:b + 1], scale=rstd[:, b:b + 1])
            last.then_inc(ready, 1)

        def apply_gnn(act, p, a):
            wait_reached(act, first_t_done, per_chunk(p, a, 0) - 1)
            wait_reached(act, first_h_lo_ready, per_group(p, a) - 1)
            act.wait_ge(ln_step["gnn"], per_group(p, a) * LN_STEPS)
            norm("gnn", x_in[a], relu_gnn, relu_gnn_ready)
            wait_reached(act, nb_done, per_gate(p - 1, a, 2, 1))
            act.wait_ge(relu_gnn_ready, per_group(p, a))
            for c in range(KC):
                last = nc.scalar.activation(h_hi[a][:, c], relu_gnn[:, :, c * P:(c + 1) * P], ACT.Copy,
                                            scale=HSCALE)
            last.then_inc(first_h_hi_ready, 1)

        def norm_factors(pool, kind, p, a, last_read):
            base = (per_group(p, a) - 1) * LN_STEPS
            st = stats[kind]
            total, gap, m2, gap2, gap2_4, m2_d, var, rstd, scaled, shift, var_eps = ln[kind]
            step = ln_step[kind]
            pool.wait_ge(stats_ready[kind], per_group(p, a))
            wait_reached(pool, last_read, per_group(p, a) - 1)
            nc.gpsimd.tensor_tensor(total, st[:, :, 1], st[:, :, 4], ALU.add).then_inc(step, 1)
            nc.gpsimd.tensor_tensor(gap, st[:, :, 1], st[:, :, 4], ALU.subtract).then_inc(step, 1)
            nc.gpsimd.tensor_tensor(m2, st[:, :, 2], st[:, :, 5], ALU.add).then_inc(step, 1)
            pool.wait_ge(step, base + 2)
            nc.gpsimd.tensor_tensor(scaled, total, minus_half, ALU.mult)
            nc.gpsimd.tensor_tensor(gap2, gap, gap, ALU.mult).then_inc(step, 1)
            pool.wait_ge(step, base + 3)
            nc.gpsimd.tensor_tensor(m2_d, m2, per_d, ALU.mult).then_inc(step, 1)
            pool.wait_ge(step, base + 4)
            nc.gpsimd.tensor_tensor(gap2_4, gap2, quarter, ALU.mult).then_inc(step, 1)
            pool.wait_ge(step, base + 6)
            nc.gpsimd.tensor_tensor(var, gap2_4, m2_d, ALU.add).then_inc(step, 1)
            pool.wait_ge(step, base + 7)
            nc.gpsimd.tensor_tensor(var_eps, var, eps, ALU.add).then_inc(step, 1)
            pool.wait_ge(step, base + 8)
            nc.gpsimd.tensor_tensor(rstd, var_eps, minus_half, ALU.pow).then_inc(step, 1)
            pool.wait_ge(step, base + 9)
            nc.gpsimd.tensor_tensor(shift, scaled, rstd, ALU.mult).then_inc(step, 1)

        with ExitStack() as setup:
            def tmp(name, shape, dtype=F32):
                return setup.enter_context(nc.sbuf_tensor(name, shape, dtype))

            raw_ih = tmp("raw_ih", [P, GATES, D])
            raw_hh = tmp("raw_hh", [P, GATES, D])
            raw_w = tmp("raw_w", [P, LAYERS, KC, D])
            raw_att = tmp("raw_att", [P, KC, D])
            att_col = tmp("att_col", [P, 2, KC])
            ih_t = tmp("ih_t", [P, KC, 3 * D])
            w_t = tmp("w_t", [P, LAYERS, KC, D])
            banks = [setup.enter_context(nc.psum_tensor(f"setup_bank{i}", [P, 512], F32)) for i in range(4)]
            LOADS = ("ih", "w", "hh", "att", "col", "bih", "bhh")
            loaded = {what: setup.enter_context(nc.semaphore(f"{what}_loaded")) for what in LOADS}
            ident_ready = setup.enter_context(nc.semaphore("ident_ready"))
            bank_full = setup.enter_context(nc.semaphore("bank_full"))
            hi_ready = setup.enter_context(nc.semaphore("hi_ready"))
            bank_read = setup.enter_context(nc.semaphore("bank_read"))
            bias_step = setup.enter_context(nc.semaphore("bias_step"))

            fills = [("ih", k, half) for k in range(KC) for half in range(2)]
            fills += [("w", layer, k) for layer in range(LAYERS) for k in range(KC)]
            fills += [("hh", k, part) for k in range(KC) for part in range(2)]
            fills += [("att", k, 0) for k in range(KC)]
            plain = len([f for f in fills if f[0] in ("ih", "w")])
            fills += [("wi", (layer, k), part) for layer in range(LAYERS) for k in range(KC) for part in range(2)]
            COLS = (slice(0, 2 * D), slice(2 * D, 3 * D))
            HALF = (slice(0, 3 * P), slice(3 * P, 6 * P))

            with nc.Block() as block:
                @block.sync
                def _(sp):
                    sp.dma_start(raw_ih[:], w_ih.rearrange("(c p) e -> p c e", p=P)).then_inc(loaded["ih"], 16)
                    sp.dma_start(raw_w[:], weight.rearrange("l (c p) e -> p l c e", p=P)).then_inc(loaded["w"], 16)
                    sp.dma_start(raw_hh[:], w_hh.rearrange("(c p) e -> p c e", p=P)).then_inc(loaded["hh"], 16)
                    sp.dma_start(raw_att[:], att_w.rearrange("(c p) f -> p c f", p=P)).then_inc(loaded["att"], 16)
                    load_gnn(sp, 0, 0)
                    with nc.allow_non_contiguous_dma(reason="small vectors, once"):
                        sp.dma_start(att_col[:], att_a.rearrange("o (w k p) -> p (o w) k", w=2, p=P)).then_inc(loaded["col"], 16)
                        sp.dma_start(bih[:], b_ih.rearrange("(c p) -> p c", p=P)).then_inc(loaded["bih"], 16)
                        sp.dma_start(bhh[:], b_hh.rearrange("(c p) -> p c", p=P)).then_inc(loaded["bhh"], 16)
                    load_gnn(sp, 0, 1)

                @block.gpsimd
                def _(pool):
                    nc.gpsimd.memset(ident[:], 0.0).then_inc(ident_ready, 1)
                    nc.gpsimd.memset(quarter, 0.25)
                    nc.gpsimd.memset(per_d, 1.0 / D)
                    nc.gpsimd.memset(eps, EPS)
                    nc.gpsimd.memset(minus_half, -0.5).then_inc(ident_ready, 1)
                    pool.wait_ge(ident_ready, 2)
                    nc.gpsimd.affine_select(out=ident[:], in_=ident[:], compare_op=ALU.not_equal, fill=1.0, base=0,
                                            pattern=[[-1, P]], channel_multiplier=1).then_inc(ident_ready, 1)
                    norm_factors(pool, "gnn", 0, 0, relu_gnn_ready)

                @block.tensor
                def _(pe):
                    pe.wait_ge(ident_ready, 3)
                    for n, (what, where, which) in enumerate(fills):
                        bank = banks[n % 4]
                        if what in loaded:
                            pe.wait_ge(loaded[what], 16)
                        if n >= 4:
                            pe.wait_ge(bank_read, n - 3)
                        if what == "ih":
                            for j in range(3):
                                last = nc.tensor.transpose(bank[:, j * P:(j + 1) * P],
                                                           raw_ih[:, 3 * which + j, where * P:(where + 1) * P], ident[:])
                        elif what == "w":
                            for j in range(KC):
                                last = nc.tensor.transpose(bank[:, j * P:(j + 1) * P],
                                                           raw_w[:, where, j, which * P:(which + 1) * P], ident[:])
                        elif what == "hh":
                            for j in range(4 if which == 0 else 2):
                                last = nc.tensor.transpose(bank[:, j * P:(j + 1) * P],
                                                           raw_hh[:, 4 * which + j, where * P:(where + 1) * P], ident[:])
                        elif what == "att":
                            for j in range(KC):
                                last = nc.tensor.transpose(bank[:, j * P:(j + 1) * P],
                                                           raw_att[:, j, where * P:(where + 1) * P], ident[:])
                            pe.wait_ge(loaded["col"], 16)
                            for j in range(KC):
                                last = nc.tensor.matmul(bank[:, D:D + 2], raw_att[:, j, where * P:(where + 1) * P],
                                                        att_col[:, :, j], start=(j == 0), stop=(j == KC - 1))
                        else:
                            layer, k = where
                            cols = COLS[which]
                            pe.wait_ge(bank_read, plain)
                            for e in range(KC):
                                last = nc.tensor.matmul(bank[:, 0:cols.stop - cols.start],
                                                        w_t[:, layer, e, k * P:(k + 1) * P], ih_t[:, e, cols],
                                                        start=(e == 0), stop=(e == KC - 1))
                        last.then_inc(bank_full, 1)

                def split_target(what, where, which):
                    if what == "hh":
                        return wh_hi[:, where, COLS[which]], wh_lo[:, where, COLS[which]], (0.5 if which else 1.0)
                    if what == "att":
                        return wa_hi[:, where, :], wa_lo[:, where, :], 1.0
                    layer, k = where
                    return wi_hi[:, layer, k, COLS[which]], wi_lo[:, layer, k, COLS[which]], 1.0

                @block.scalar
                def _(act):
                    for n, fill in enumerate(fills):
                        if fill[0] in ("ih", "w"):
                            continue
                        hi, _, scale = split_target(*fill)
                        act.wait_ge(bank_full, n + 1)
                        nc.scalar.activation(hi, banks[n % 4][:, 0:hi.shape[-1]], ACT.Copy,
                                             scale=scale).then_inc(hi_ready, 1)
                        if n == plain + 11:
                            apply_gnn(act, 0, 0)

                @block.vector
                def _(dve):
                    for n, (what, where, which) in enumerate(fills):
                        dve.wait_ge(bank_full, n + 1)
                        bank = banks[n % 4]
                        if what == "ih":
                            nc.vector.tensor_copy(ih_t[:, where, HALF[which]], bank[:, 0:3 * P]).then_inc(bank_read, 1)
                        elif what == "w":
                            nc.vector.tensor_copy(w_t[:, where, which, :], bank[:, 0:D]).then_inc(bank_read, 1)
                        else:
                            hi, lo, scale = split_target(what, where, which)
                            dve.wait_ge(hi_ready, n - plain + 1)
                            nc.vector.scalar_tensor_tensor(lo, bank[:, 0:lo.shape[-1]], scale, hi.bitcast(F32),
                                                           ALU.mult, ALU.subtract).then_inc(bank_read, 1)
                        if n == plain + 7:
                            stats_gnn(dve, 0, 0)
                        if n == plain + 12:
                            split_gnn(dve, 0, 0)
                    for what in ("bih", "bhh"):
                        dve.wait_ge(loaded[what], 16)
                    nc.vector.tensor_tensor(b_rz[:], bih[:, 0:4], bhh[:, 0:4], ALU.add).then_inc(bias_step, 1)
                    dve.wait_ge(bias_step, 1)
                    nc.vector.tensor_scalar(b_rz[:], b_rz[:], 0.5, None, ALU.mult)
                    nc.vector.tensor_scalar(b_hn[:], bhh[:, 4:6], 0.5, None, ALU.mult)

        x_res = both("x_res", [P, GROUP, D], F32)
        adj_att = both("adj_att", [P, GROUP, P], I32)
        ht = both("ht", [P, KC, T], F32)
        ht_hi = [both(f"ht_hi{q}_", [P, KC, T], F32R) for q in range(2)]
        ht_lo = [both(f"ht_lo{q}_", [P, KC, T], F32R) for q in range(2)]
        nb_hi = both("nb_hi", [P, KC, T], F32R)
        nb_lo = both("nb_lo", [P, KC, T], F32R)
        wh_out_hi = both("wh_out_hi", [P, GROUP, D], F32R)
        wh_out_lo = both("wh_out_lo", [P, GROUP, D], F32R)
        s12 = both("s12", [P, GROUP, 2], F32)
        row_scale = both("row_scale", [P, GROUP], F32)
        relu_att = sb("relu_att", [P, GROUP, D], F32)
        ut_hi = sb("ut_hi", [P, KC, T], F32R)
        ut_lo = sb("ut_lo", [P, KC, T], F32R)
        hn_b = [sb(f"hn_b{c}", [P, T], F32) for c in range(2)]
        tanh_r = [sb(f"tanh_r{c}", [P, T], F32) for c in range(2)]
        tanh_z = [sb(f"tanh_z{c}", [P, T], F32) for c in range(2)]
        n_pre = [sb(f"n_pre{c}", [P, T], F32) for c in range(2)]
        n_out = [sb(f"n_out{c}", [P, T], F32) for c in range(2)]
        diff = [sb(f"diff{c}", [P, T], F32) for c in range(2)]
        score = sb("score", [P, GROUP, P], F32)
        prob = sb("prob", [P, GROUP, P], F32)
        pt_hi = sb("pt_hi", [P, GROUP, P], F32R)
        pt_lo = sb("pt_lo", [P, GROUP, P], F32R)
        row_max = sb("row_max", [P, GROUP], F32)
        minus_max = sb("minus_max", [P, GROUP], F32)
        row_sum = sb("row_sum", [P, GROUP], F32)
        row_inv = sb("row_inv", [P, GROUP], F32)

        def bank(name):
            return ctx.enter_context(nc.psum_tensor(name, [P, 512], F32))

        hn_bank, r_bank, in_bank, z_bank = bank("hn_bank"), bank("r_bank"), bank("in_bank"), bank("z_bank")
        nb_bank, t_bank, w_bank, s_bank = bank("nb_bank"), bank("t_bank"), bank("w_bank"), bank("s_bank")

        def project_bank(p, b):
            return (w_bank, hn_bank, r_bank, in_bank)[b] if isinstance(p, int) and p == pairs - 1 else w_bank

        def attend_bank(p, half):
            return (z_bank, nb_bank)[half] if isinstance(p, int) and p == pairs - 1 else w_bank

        x_res_loaded = [sem(f"x_res_loaded{a}") for a in range(2)]
        adj_att_loaded = [sem(f"adj_att_loaded{a}") for a in range(2)]
        out_stored = [sem(f"out_stored{a}") for a in range(2)]
        hn_done, r_done, in_done, z_done = sem("hn_done"), sem("r_done"), sem("in_done"), sem("z_done")
        t_done, res_t_done, att_t_done = sem("t_done"), sem("res_t_done"), sem("att_t_done")
        wh_done, s2_done, probs_t_done, attend_done = (sem("wh_done"), sem("s2_done"), sem("probs_t_done"),
                                                       sem("attend_done"))
        hn_ready, tanh_r_ready, n_ready, tanh_z_ready = (sem("hn_ready"), sem("tanh_r_ready"), sem("n_ready"),
                                                         sem("tanh_z_ready"))
        ht_hi_ready, first_ht_hi_ready = sem("ht_hi_ready"), sem("first_ht_hi_ready")
        h_hi_ready = sem("h_hi_ready")
        nb_hi_ready = sem("nb_hi_ready")
        relu_att_ready = sem("relu_att_ready")
        ut_hi_ready, wh_hi_ready, prob_ready, pt_hi_ready = (sem("ut_hi_ready"), sem("wh_hi_ready"),
                                                             sem("prob_ready"), sem("pt_hi_ready"))
        rn_ready, n_pre_ready, diff_ready, zdiff_ready, h_ready = (sem("rn_ready"), sem("n_pre_ready"),
                                                                   sem("diff_ready"), sem("zdiff_ready"),
                                                                   sem("h_ready"))
        ht_lo_ready, first_ht_lo_ready = sem("ht_lo_ready"), sem("first_ht_lo_ready")
        h_lo_ready = sem("h_lo_ready")
        nb_lo_ready, x1_ready = sem("nb_lo_ready"), sem("x1_ready")
        ut_lo_ready, wh_lo_ready, pt_lo_ready = sem("ut_lo_ready"), sem("wh_lo_ready"), sem("pt_lo_ready")
        mask_ready, sum_ready, leaky_ready, masked_ready, max_ready, minus_max_ready = (
            sem("mask_ready"), sem("sum_ready"), sem("leaky_ready"), sem("masked_ready"), sem("max_ready"),
            sem("minus_max_ready"))
        inv_ready, row_scale_ready, out_ready = sem("inv_ready"), sem("row_scale_ready"), sem("out_ready")

        def slots(p, gate, side):
            for slot in range(2 * LAYERS):
                for step in range(len(STEPS)):
                    gate(p, slot % 2, slot // 2, STEPS[step][:-1], step // 4)
                    for stage, *which, offset in SIDE.get((slot, step), ()):
                        if stage in side and exists(p + offset):
                            side[stage](p + offset, *which)

        def all_pairs(engine, gate, side):
            for stage, *which in HEAD:
                if stage in side:
                    side[stage](0, *which)
            slots(0, gate, side)
            with engine.Fori(1, pairs - 1) as p:
                slots(p, gate, side)
            slots(pairs - 1, gate, side)
            for stage, *which in TAIL:
                if stage in side:
                    side[stage](pairs - 1, *which)

        with nc.Block() as block:
            @block.sync
            def _(sp):
                def store(p, a):
                    index = sp.snap(p * 2 + a)
                    sp.wait_ge(out_ready, per_chunk(p, a, 1))
                    sp.dma_start(dram_group(out_v, index), x_res[a][:]).then_inc(out_stored[a], 16)

                def load_att(p, a):
                    index = sp.snap(p * 2 + a)
                    wait_reached(sp, out_stored[a], per_load(p - 1))
                    sp.dma_start(x_res[a][:], dram_group(x_v, index)).then_inc(x_res_loaded[a], 16)
                    wait_reached(sp, mask_ready, per_group(p - 1, a))
                    sp.dma_start(adj_att[a][:], dram_group(adj_v, index)).then_inc(adj_att_loaded[a], 16)

                def pair(p):
                    for a in range(2):
                        if exists(p + 1):
                            load_gnn(sp, p + 1, a)
                    for a in range(2):
                        if exists(p - 1):
                            store(p - 1, a)
                        load_att(p, a)

                pair(0)
                with sp.Fori(1, pairs - 1) as p:
                    pair(p)
                pair(pairs - 1)
                for a in range(2):
                    store(pairs - 1, a)
                for a in range(2):
                    sp.wait_ge(out_stored[a], per_load(pairs - 1))

            @block.tensor
            def _(pe):
                def products(bank_ap, terms):
                    todo = [m for w_hi, w_lo, d_hi, d_lo in terms for m in ((w_hi, d_hi), (w_hi, d_lo), (w_lo, d_hi))]
                    for i, (w, d) in enumerate(todo):
                        last = nc.tensor.matmul(bank_ap, w, d, start=(i == 0), stop=(i == len(todo) - 1))
                    return last

                def gate(p, a, layer, name, c):
                    n = per_gate(p, a, layer, c)
                    row = {"hn": 4, "r": 0, "in": 4, "z": 2}[name] + c
                    cols = slice(row * P, (row + 1) * P)
                    from_h = [(wh_hi[:, k, cols], wh_lo[:, k, cols], ht_hi[layer % 2][a][:, k, :],
                               ht_lo[layer % 2][a][:, k, :]) for k in range(KC)]
                    from_nb = [(wi_hi[:, layer, k, cols], wi_lo[:, layer, k, cols], nb_hi[a][:, k, :],
                                nb_lo[a][:, k, :]) for k in range(KC)]
                    if name == "hn":
                        if c == 0 and layer == 0:
                            pe.wait_ge(first_ht_lo_ready, per_chunk(p, a, 1))
                        elif c == 0:
                            pe.wait_ge(ht_lo_ready, per_later_layer(p, a, layer, 1))
                        wait_reached(pe, hn_ready, n - 1)
                        products(hn_bank[:], from_h).then_inc(hn_done, 1)
                    elif name == "r":
                        wait_reached(pe, tanh_r_ready, n - 1)
                        if c == 0:
                            pe.wait_ge(nb_lo_ready, per_gate(p, a, layer, 1))
                        products(r_bank[:], from_h + from_nb).then_inc(r_done, 1)
                    elif name == "in":
                        wait_reached(pe, n_pre_ready, n - 1)
                        products(in_bank[:], from_nb).then_inc(in_done, 1)
                    else:
                        wait_reached(pe, tanh_z_ready, n - 1)
                        products(z_bank[:], from_h + from_nb).then_inc(z_done, 1)

                def group_transposes(source, blocks):
                    for b in range(GROUP):
                        last = nc.tensor.transpose(t_bank[:, b * P:(b + 1) * P], blocks(source, b), ident[:])
                    return last

                def columns_of(source, b):
                    return source[:, b * P:(b + 1) * P]

                def first_transpose(p, a, c):
                    pe.wait_ge(relu_gnn_ready, per_group(p, a))
                    wait_reached(pe, first_ht_lo_ready, per_chunk(p, a, c) - 1)
                    wait_reached(pe, x1_ready, per_chunk(p - 1, a, c))
                    group_transposes(relu_gnn, lambda s, b: s[:, b, c * P:(c + 1) * P]).then_inc(first_t_done, 1)

                def transpose(p, a, layer, c):
                    pe.wait_ge(h_ready, per_gate(p, a, layer - 1, c))
                    wait_reached(pe, h_lo_ready, per_later_layer(p, a, layer, c) - 1)
                    if layer == 1 and a == 0 and c == 0:
                        pe.wait_ge(first_ht_lo_ready, per_chunk(p, 1, 1))
                    if layer == 1 and (a, c) != (0, 1):
                        before = {(0, 0): (0, 1), (1, 0): (1, 0), (1, 1): (1, 1)}[a, c]
                        wait_reached(pe, ut_lo_ready, per_chunk(p - 1, *before))
                    group_transposes(ht[a][:, c, :], columns_of).then_inc(t_done, 1)

                def residual(p, a, c):
                    pe.wait_ge(h_ready, per_gate(p, a, LAYERS - 1, c))
                    wait_reached(pe, x1_ready, per_chunk(p, a, c) - 1)
                    if a == 0 and c == 0:
                        pe.wait_ge(h_lo_ready, per_later_layer(p, 1, 2, 1))
                    if exists(p + 1) and (a, c) != (0, 0):
                        before = (0, 0) if a == 0 else ((0, 1) if c == 0 else (1, 0))
                        pe.wait_ge(first_ht_lo_ready, per_chunk(p + 1, *before))
                    group_transposes(ht[a][:, c, :], columns_of).then_inc(res_t_done, 1)

                def att_transpose(p, a, c):
                    pe.wait_ge(relu_att_ready, per_group(p, a))
                    wait_reached(pe, ut_lo_ready, per_chunk(p, a, c) - 1)
                    if a == 0 and c == 0:
                        pe.wait_ge(x1_ready, per_chunk(p, 1, 1))
                        if exists(p + 1):
                            pe.wait_ge(first_ht_lo_ready, per_chunk(p + 1, 1, 1))
                    if a == 1 and exists(p + 1):
                        before = (0, 1) if c == 0 else (1, 0)
                        pe.wait_ge(h_lo_ready, per_later_layer(p + 1, before[0], 1, before[1]))
                    group_transposes(relu_att, lambda s, b: s[:, b, c * P:(c + 1) * P]).then_inc(att_t_done, 1)

                def neighbours(p, a, layer, c):
                    n = per_gate(p, a, layer, c)
                    if layer == 0:
                        pe.wait_ge(first_h_lo_ready, per_group(p, a))
                        pe.wait_ge(adj_s_ready, per_group(p, a))
                    else:
                        pe.wait_ge(h_lo_ready, per_later_layer(p, a, layer, c))
                    wait_reached(pe, nb_lo_ready, n - 1)
                    for b in range(GROUP):
                        block_ap = nb_bank[:, b * P:(b + 1) * P]
                        nc.tensor.matmul(block_ap, h_hi[a][:, c, b, :], adj_s[a][:, b, :], start=True, stop=False)
                        last = nc.tensor.matmul(block_ap, h_lo[a][:, c, b, :], adj_s[a][:, b, :],
                                                start=False, stop=True)
                    last.then_inc(nb_done, 1)

                def project(p, a, b):
                    n = per_graph(p, a, b)
                    pe.wait_ge(ut_lo_ready, per_chunk(p, a, 1))
                    last_pair = project_bank(p, 1) is not w_bank
                    wait_reached(pe, wh_lo_ready, n - 4 if last_pair else n - 1)
                    if a == 0 and b == 0:
                        wait_reached(pe, out_ready, per_chunk(p - 1, 1, 1))
                    if last_pair and a == 0 and b == 0:
                        pe.wait_ge(hn_ready, per_gate(p, 1, LAYERS - 1, 1))
                        pe.wait_ge(tanh_r_ready, per_gate(p, 1, LAYERS - 1, 1))
                        pe.wait_ge(n_pre_ready, per_gate(p, 1, LAYERS - 1, 1))
                    nodes = slice(b * P, (b + 1) * P)
                    products(project_bank(p, b)[:, 0:D + 2],
                             [(ut_hi[:, k, nodes], ut_lo[:, k, nodes], wa_hi[:, k, :], wa_lo[:, k, :])
                              for k in range(KC)]).then_inc(wh_done, 1)

                def scores(p, a):
                    pe.wait_ge(wh_lo_ready, per_graph(p, a, GROUP - 1))
                    wait_reached(pe, pt_lo_ready, per_group(p, a) - 1)
                    for b in range(GROUP):
                        last = nc.tensor.transpose(s_bank[:, b * P:(b + 1) * P],
                                                   s12[a][:, b, 1:2].broadcast_to([P, P]), ident[:])
                    last.then_inc(s2_done, 1)

                def probs_transpose(p, a):
                    pe.wait_ge(prob_ready, per_group(p, a))
                    for b in range(GROUP):
                        last = nc.tensor.transpose(s_bank[:, b * P:(b + 1) * P], prob[:, b, :], ident[:])
                    last.then_inc(probs_t_done, 1)

                def attend(p, a, half):
                    n = per_chunk(p, a, half)
                    pe.wait_ge(pt_lo_ready, per_group(p, a))
                    pe.wait_ge(wh_lo_ready, per_graph(p, a, GROUP - 1))
                    last_pair = attend_bank(p, half) is not w_bank
                    if last_pair and a == 0:
                        pe.wait_ge(tanh_z_ready, per_gate(p, 1, LAYERS - 1, 1))
                        pe.wait_ge(nb_lo_ready, per_gate(p, 1, LAYERS - 1, 1))
                    else:
                        wait_reached(pe, out_ready, n - 2 if last_pair else n - 1)
                    if a == 0 and half == 0:
                        pe.wait_ge(wh_lo_ready, per_graph(p, 1, GROUP - 1))
                    for i in range(2):
                        b = 2 * half + i
                        last = products(attend_bank(p, half)[:, i * D:(i + 1) * D],
                                        [(pt_hi[:, b, :], pt_lo[:, b, :], wh_out_hi[a][:, b, :], wh_out_lo[a][:, b, :])])
                    last.then_inc(attend_done, 1)

                all_pairs(pe, gate, {
                    "first_transpose": first_transpose, "transpose": transpose, "residual": residual,
                    "att_transpose": att_transpose, "neighbours": neighbours, "project": project, "scores": scores,
                    "probs_transpose": probs_transpose, "attend": attend})

            @block.scalar
            def _(act):
                def gate(p, a, layer, name, c):
                    n = per_gate(p, a, layer, c)
                    if name == "hn":
                        act.wait_ge(hn_done, n)
                        wait_reached(act, rn_ready, n - 2)
                        nc.scalar.activation(hn_b[c][:], hn_bank[:], ACT.Identity,
                                             bias=b_hn[:, c:c + 1]).then_inc(hn_ready, 1)
                    elif name == "r":
                        act.wait_ge(r_done, n)
                        wait_reached(act, rn_ready, n - 2)
                        nc.scalar.activation(tanh_r[c][:], r_bank[:], ACT.Tanh, bias=b_rz[:, c:c + 1],
                                             scale=0.5).then_inc(tanh_r_ready, 1)
                    elif name == "z":
                        act.wait_ge(n_pre_ready, n)
                        wait_reached(act, h_ready, n - 2)
                        nc.scalar.activation(n_out[c][:], n_pre[c][:], ACT.Tanh,
                                             bias=bih[:, 4 + c:5 + c]).then_inc(n_ready, 1)
                        act.wait_ge(z_done, n)
                        wait_reached(act, zdiff_ready, n - 2)
                        nc.scalar.activation(tanh_z[c][:], z_bank[:], ACT.Tanh, bias=b_rz[:, 2 + c:3 + c],
                                             scale=0.5).then_inc(tanh_z_ready, 1)

                def split_state(p, a, layer, c):
                    act.wait_ge(h_ready, per_gate(p, a, layer - 1, c))
                    nc.scalar.activation(ht_hi[layer % 2][a][:, c, :], ht[a][:, c, :],
                                         ACT.Copy).then_inc(ht_hi_ready, 1)

                def apply_att(p, a):
                    wait_reached(act, att_t_done, per_chunk(p, a, 0) - 1)
                    act.wait_ge(ln_step["att"], per_group(p, a) * LN_STEPS)
                    norm("att", x_res[a], relu_att, relu_att_ready)

                def first_transpose(p, a, c):
                    act.wait_ge(first_t_done, per_chunk(p, a, c))
                    nc.scalar.activation(ht[a][:, c, :], t_bank[:], ACT.Copy)
                    nc.scalar.activation(ht_hi[0][a][:, c, :], t_bank[:], ACT.Copy).then_inc(first_ht_hi_ready, 1)

                def transpose(p, a, layer, c):
                    act.wait_ge(t_done, per_later_layer(p, a, layer, c))
                    nc.scalar.activation(h_hi[a][:, c].rearrange("p b t -> p (b t)"), t_bank[:], ACT.Copy,
                                         scale=HSCALE).then_inc(h_hi_ready, 1)

                def neighbours(p, a, layer, c):
                    act.wait_ge(nb_done, per_gate(p, a, layer, c))
                    nc.scalar.activation(nb_hi[a][:, c, :], nb_bank[:], ACT.Copy).then_inc(nb_hi_ready, 1)

                def att_transpose(p, a, c):
                    act.wait_ge(att_t_done, per_chunk(p, a, c))
                    wait_reached(act, wh_done, per_graph(p, a, 0) - 1)
                    nc.scalar.activation(ut_hi[:, c, :], t_bank[:], ACT.Copy).then_inc(ut_hi_ready, 1)

                def project(p, a, b):
                    act.wait_ge(wh_done, per_graph(p, a, b))
                    nc.scalar.activation(wh_out_hi[a][:, b, :], project_bank(p, b)[:, 0:D], ACT.Copy).then_inc(wh_hi_ready, 1)

                def softmax(p, a):
                    act.wait_ge(minus_max_ready, per_group(p, a))
                    wait_reached(act, probs_t_done, per_group(p, a) - 1)
                    for b in range(GROUP):
                        last = nc.scalar.activation(prob[:, b, :], score[:, b, :], ACT.Exp,
                                                    bias=minus_max[:, b:b + 1], accum_out=row_sum[:, b:b + 1])
                    last.then_inc(prob_ready, 1)

                def probs_transpose(p, a):
                    act.wait_ge(probs_t_done, per_group(p, a))
                    nc.scalar.activation(pt_hi[:].rearrange("p b t -> p (b t)"), s_bank[:],
                                         ACT.Copy).then_inc(pt_hi_ready, 1)

                all_pairs(act, gate, {
                    "apply_gnn": lambda p, a: apply_gnn(act, p, a), "apply_att": apply_att, "split_state": split_state,
                    "first_transpose": first_transpose, "transpose": transpose, "att_transpose": att_transpose,
                    "neighbours": neighbours, "project": project, "softmax": softmax,
                    "probs_transpose": probs_transpose})

            @block.vector
            def _(dve):
                def low_part(lo, whole, hi, ready):
                    nc.vector.tensor_tensor(lo, whole, hi.bitcast(F32), ALU.subtract).then_inc(ready, 1)

                def gate(p, a, layer, name, c):
                    n = per_gate(p, a, layer, c)
                    if name == "r":
                        dve.wait_ge(hn_ready, n)
                        dve.wait_ge(tanh_r_ready, n)
                        wait_reached(dve, n_ready, n - 2)
                        nc.vector.scalar_tensor_tensor(n_pre[c][:], tanh_r[c][:], 1.0, hn_b[c][:], ALU.add,
                                                       ALU.mult).then_inc(rn_ready, 1)
                    elif name == "in":
                        dve.wait_ge(rn_ready, n)
                        dve.wait_ge(in_done, n)
                        nc.vector.tensor_tensor(n_pre[c][:], n_pre[c][:], in_bank[:], ALU.add).then_inc(n_pre_ready, 1)

                def update(p, a, layer, c):
                    n = per_gate(p, a, layer, c)
                    dve.wait_ge(n_ready, n)
                    wait_reached(dve, h_ready, n - 2)
                    nc.vector.tensor_tensor(diff[c][:], ht[a][:, c, :], n_out[c][:], ALU.subtract).then_inc(diff_ready, 1)
                    dve.wait_ge(diff_ready, n)
                    dve.wait_ge(tanh_z_ready, n)
                    nc.vector.scalar_tensor_tensor(diff[c][:], tanh_z[c][:], 1.0, diff[c][:], ALU.add,
                                                   ALU.mult).then_inc(zdiff_ready, 1)
                    dve.wait_ge(zdiff_ready, n)
                    nc.vector.scalar_tensor_tensor(ht[a][:, c, :], diff[c][:], 0.5, n_out[c][:], ALU.mult,
                                                   ALU.add).then_inc(h_ready, 1)

                def split_state(p, a, layer, c):
                    q = layer % 2
                    dve.wait_ge(ht_hi_ready, per_later_layer(p, a, layer, c))
                    low_part(ht_lo[q][a][:, c, :], ht[a][:, c, :], ht_hi[q][a][:, c, :], ht_lo_ready)

                def stats_att(p, a):
                    dve.wait_ge(x1_ready, per_chunk(p, a, 1))
                    wait_reached(dve, ln_step["att"], (per_group(p, a) - 1) * LN_STEPS)
                    statistics("att", x_res[a])

                def first_transpose(p, a, c):
                    dve.wait_ge(first_ht_hi_ready, per_chunk(p, a, c))
                    low_part(ht_lo[0][a][:, c, :], t_bank[:], ht_hi[0][a][:, c, :], first_ht_lo_ready)

                def transpose(p, a, layer, c):
                    dve.wait_ge(h_hi_ready, per_later_layer(p, a, layer, c))
                    nc.vector.scalar_tensor_tensor(h_lo[a][:, c].rearrange("p b t -> p (b t)"), t_bank[:], HSCALE,
                                                   h_hi[a][:, c].rearrange("p b t -> p (b t)"), ALU.mult,
                                                   ALU.subtract).then_inc(h_lo_ready, 1)

                def residual(p, a, c):
                    dve.wait_ge(x_res_loaded[a], per_load(p))
                    dve.wait_ge(res_t_done, per_chunk(p, a, c))
                    part = x_res[a][:, :, c * P:(c + 1) * P]
                    nc.vector.tensor_tensor(part, part, t_bank[:].rearrange("p (b t) -> p b t", b=GROUP),
                                            ALU.add).then_inc(x1_ready, 1)

                def neighbours(p, a, layer, c):
                    dve.wait_ge(nb_hi_ready, per_gate(p, a, layer, c))
                    low_part(nb_lo[a][:, c, :], nb_bank[:], nb_hi[a][:, c, :], nb_lo_ready)

                def att_transpose(p, a, c):
                    dve.wait_ge(ut_hi_ready, per_chunk(p, a, c))
                    low_part(ut_lo[:, c, :], t_bank[:], ut_hi[:, c, :], ut_lo_ready)

                def project(p, a, b):
                    dve.wait_ge(wh_hi_ready, per_graph(p, a, b))
                    nc.vector.tensor_copy(s12[a][:, b, :], project_bank(p, b)[:, D:D + 2])
                    low_part(wh_out_lo[a][:, b, :], project_bank(p, b)[:, 0:D], wh_out_hi[a][:, b, :], wh_lo_ready)

                def scores(p, a):
                    n = per_group(p, a)
                    dve.wait_ge(adj_att_loaded[a], per_load(p))
                    wait_reached(dve, probs_t_done, n - 1)
                    nc.vector.tensor_scalar(prob[:], adj_att[a][:], 0.0, MASKED, ALU.is_equal,
                                            ALU.mult).then_inc(mask_ready, 1)
                    dve.wait_ge(s2_done, n)
                    wait_reached(dve, prob_ready, n - 1)
                    nc.vector.tensor_tensor(score[:], s_bank[:].rearrange("p (b t) -> p b t", b=GROUP),
                                            s12[a][:, :, 0:1].broadcast_to([P, GROUP, P]),
                                            ALU.add).then_inc(sum_ready, 1)
                    dve.wait_ge(sum_ready, n)
                    nc.vector.scalar_tensor_tensor(score[:], score[:], ALPHA, score[:], ALU.mult,
                                                   ALU.max).then_inc(leaky_ready, 1)
                    dve.wait_ge(leaky_ready, n)
                    dve.wait_ge(mask_ready, n)
                    nc.vector.tensor_tensor(score[:], score[:], prob[:], ALU.add).then_inc(masked_ready, 1)
                    dve.wait_ge(masked_ready, n)
                    nc.vector.tensor_reduce(row_max[:], score[:], AX_X, ALU.max).then_inc(max_ready, 1)
                    dve.wait_ge(max_ready, n)
                    nc.vector.tensor_scalar(minus_max[:], row_max[:], -1.0, None, ALU.mult).then_inc(minus_max_ready, 1)

                def probs_transpose(p, a):
                    n = per_group(p, a)
                    dve.wait_ge(prob_ready, n)
                    nc.vector.reciprocal(row_inv[:], row_sum[:]).then_inc(inv_ready, 1)
                    dve.wait_ge(inv_ready, n)
                    nc.vector.scalar_tensor_tensor(row_scale[a][:], row_max[:], 0.5 * MASKED, row_inv[:], ALU.is_gt,
                                                   ALU.mult).then_inc(row_scale_ready, 1)
                    dve.wait_ge(pt_hi_ready, n)
                    low_part(pt_lo[:].rearrange("p b t -> p (b t)"), s_bank[:],
                             pt_hi[:].rearrange("p b t -> p (b t)"), pt_lo_ready)

                def attend(p, a, half):
                    dve.wait_ge(attend_done, per_chunk(p, a, half))
                    dve.wait_ge(row_scale_ready, per_group(p, a))
                    for i in range(2):
                        b = 2 * half + i
                        last = nc.vector.scalar_tensor_tensor(x_res[a][:, b, :], attend_bank(p, half)[:, i * D:(i + 1) * D],
                                                              row_scale[a][:, b:b + 1], x_res[a][:, b, :], ALU.mult,
                                                              ALU.add)
                    last.then_inc(out_ready, 1)

                all_pairs(dve, gate, {
                    "stats_gnn": lambda p, a: stats_gnn(dve, p, a), "split_gnn": lambda p, a: split_gnn(dve, p, a),
                    "stats_att": stats_att,
                    "update": update, "split_state": split_state, "first_transpose": first_transpose,
                    "transpose": transpose, "residual": residual, "att_transpose": att_transpose,
                    "neighbours": neighbours, "project": project, "scores": scores,
                    "probs_transpose": probs_transpose, "attend": attend})

            @block.gpsimd
            def _(pool):
                all_pairs(pool, lambda *step: None, {
                    "stats_gnn": lambda p, a: norm_factors(pool, "gnn", p, a, relu_gnn_ready),
                    "stats_att": lambda p, a: norm_factors(pool, "att", p, a, relu_att_ready)})


_INS = ["x", "adj", "L0_gnn_weight", "L0_gnn_w_ih", "L0_gnn_w_hh", "L0_gnn_b_ih", "L0_gnn_b_hh", "L1_gnn_W",
        "L1_gnn_a"]


def kernel(**inputs):
    import numpy as _np
    import concourse.bacc as _bacc
    from concourse import mybir as _mybir
    from concourse.bass_utils import run_bass_kernel_spmd as _run

    nc = _bacc.Bacc("TRN2", target_bir_lowering=False, num_devices=1)
    arrays, args = {}, []
    for name in _INS:
        a = _np.ascontiguousarray(inputs[name])
        arrays[f"in_{name}_dram"] = a
        args.append(nc.dram_tensor(f"in_{name}_dram", a.shape, _mybir.dt.from_np(a.dtype), kind="ExternalInput").ap())
    out = nc.dram_tensor("out_dram", inputs["x"].shape, _mybir.dt.float32, kind="ExternalOutput").ap()
    graph_blocks(nc, *args, out)
    r = _run(nc, [arrays], core_ids=[0])
    return r.results[0]["out_dram"]
```

```python
from contextlib import ExitStack

import concourse.bass as bass
from concourse import mybir

F32 = mybir.dt.float32
F32R = mybir.dt.float32r
F16 = mybir.dt.float16
I32 = mybir.dt.int32
ALU = mybir.AluOpType
ACT = mybir.ActivationFunctionType
AX_X = mybir.AxisListType.X

P = 128
D = 256
KC = D // P
GROUP = 4
T = GROUP * P
LAYERS = 3
GATES = 3 * KC
ALPHA = 0.2
EPS = 1e-5
MASKED = -1e30
HSCALE = 2048.0
PSCALE = 16384.0

STEPS = ("hn0", "r0", "in0", "z0", "hn1", "r1", "in1", "z1")
SIDE = {
    (0, 0): [("residual", 1, 0, -1), ("update", 1, 2, 1, -1)],
    (0, 1): [("first_transpose", 1, 0, 0)],
    (0, 2): [("neighbours", 1, 0, 0, 0)],
    (0, 3): [("residual", 1, 1, -1), ("split_att", 0, -1)],
    (0, 4): [("first_transpose", 1, 1, 0), ("update", 0, 0, 0, 0)],
    (0, 5): [("neighbours", 1, 0, 1, 0), ("dots", 0, 0, -1)],
    (0, 6): [("stats_att", 1, -1)],
    (0, 7): [("dots", 0, 1, -1)],
    (1, 0): [("update", 0, 0, 1, 0)],
    (1, 1): [("transpose", 0, 1, 0, 0)],
    (1, 2): [("split_state", 0, 1, 0, 0), ("apply_att", 1, -1)],
    (1, 3): [("transpose", 0, 1, 1, 0)],
    (1, 4): [("update", 1, 0, 0, 0), ("neighbours", 0, 1, 0, 0)],
    (1, 5): [("split_state", 0, 1, 1, 0)],
    (1, 6): [("neighbours", 0, 1, 1, 0)],
    (1, 7): [("split_att", 1, -1)],
    (2, 0): [("update", 1, 0, 1, 0)],
    (2, 1): [("transpose", 1, 1, 0, 0), ("scores", 0, -1)],
    (2, 2): [("split_state", 1, 1, 0, 0)],
    (2, 3): [("softmax", 0, -1)],
    (2, 4): [("update", 0, 1, 0, 0), ("split_state", 1, 1, 1, 0), ("neighbours", 1, 1, 0, 0)],
    (2, 5): [("transpose", 1, 1, 1, 0)],
    (2, 6): [("probs_transpose", 0, -1)],
    (2, 7): [("neighbours", 1, 1, 1, 0)],
    (3, 0): [("update", 0, 1, 1, 0)],
    (3, 1): [("transpose", 0, 2, 0, 0), ("gather", 0, 0, -1)],
    (3, 2): [("split_state", 0, 2, 0, 0), ("dots", 1, 0, -1)],
    (3, 3): [("transpose", 0, 2, 1, 0), ("gather", 0, 1, -1)],
    (3, 4): [("update", 1, 1, 0, 0), ("neighbours", 0, 2, 0, 0), ("dots", 1, 1, -1)],
    (3, 5): [("split_state", 0, 2, 1, 0), ("attend", 0, 0, -1)],
    (3, 6): [("neighbours", 0, 2, 1, 0)],
    (3, 7): [("attend", 0, 1, -1)],
    (4, 0): [("update", 1, 1, 1, 0), ("scores", 1, -1)],
    (4, 1): [("transpose", 1, 2, 0, 0)],
    (4, 2): [("split_state", 1, 2, 0, 0), ("softmax", 1, -1)],
    (4, 3): [("transpose", 1, 2, 1, 0), ("stats_gnn", 0, 1)],
    (4, 4): [("update", 0, 2, 0, 0), ("neighbours", 1, 2, 0, 0)],
    (4, 5): [("probs_transpose", 1, -1), ("split_state", 1, 2, 1, 0), ("apply_gnn", 0, 1)],
    (4, 6): [("neighbours", 1, 2, 1, 0), ("split_gnn", 0, 1)],
    (4, 7): [("gather", 1, 0, -1)],
    (5, 0): [("residual", 0, 0, 0), ("update", 0, 2, 1, 0)],
    (5, 1): [("first_transpose", 0, 0, 1), ("gather", 1, 1, -1)],
    (5, 2): [("attend", 1, 0, -1), ("neighbours", 0, 0, 0, 1), ("stats_gnn", 1, 1)],
    (5, 3): [("residual", 0, 1, 0), ("attend", 1, 1, -1)],
    (5, 4): [("first_transpose", 0, 1, 1), ("update", 1, 2, 0, 0)],
    (5, 5): [("neighbours", 0, 0, 1, 1), ("stats_att", 0, 0)],
    (5, 6): [("apply_gnn", 1, 1)],
    (5, 7): [("split_gnn", 1, 1), ("apply_att", 0, 0)],
}
SETUP_SIDE = {
    9: [("stats_gnn", 0)],
    13: [("apply_gnn", 0)],
    17: [("split_gnn", 0)],
    19: [("stats_gnn", 1)],
    22: [("first_transpose", 0, 0)],
    23: [("neighbours", 0, 0)],
    25: [("first_transpose", 0, 1)],
    27: [("neighbours", 0, 1)],
}
HEAD = [("apply_gnn", 1), ("split_gnn", 1)]
LAST_SLOT_SIDE = {
    (5, 0): [("residual", 0, 0, 0), ("update", 0, 2, 1, 0)],
    (5, 1): [("gather", 1, 1, -1), ("attend", 1, 0, -1)],
    (5, 2): [("residual", 0, 1, 0), ("stats_att", 0, 0)],
    (5, 3): [("attend", 1, 1, -1)],
    (5, 4): [("update", 1, 2, 0, 0), ("apply_att", 0, 0)],
    (5, 5): [("split_att", 0, 0)],
}
TAIL = [("update", 1, 2, 1), ("residual", 1, 0), ("residual", 1, 1), ("stats_att", 1), ("dots", 0, 0),
        ("dots", 0, 1), ("scores", 0), ("apply_att", 1), ("split_att", 1), ("softmax", 0), ("dots", 1, 0),
        ("dots", 1, 1), ("probs_transpose", 0), ("scores", 1), ("gather", 0, 0), ("gather", 0, 1),
        ("softmax", 1), ("attend", 0, 0), ("probs_transpose", 1), ("attend", 0, 1), ("gather", 1, 0),
        ("gather", 1, 1), ("attend", 1, 0), ("attend", 1, 1)]


def per_group(p, a):
    return p * 2 + a + 1


def per_chunk(p, a, c):
    return p * 4 + 2 * a + c + 1


def per_graph(p, a, b):
    return p * 8 + 4 * a + b + 1


def per_gate(p, a, layer, c):
    return p * 12 + 4 * layer + 2 * a + c + 1


def per_later_layer(p, a, layer, c):
    return p * 8 + 4 * (layer - 1) + 2 * a + c + 1


def per_load(p):
    return p * 16 + 16


def wait_reached(engine, semaphore, count):
    if not (isinstance(count, int) and count < 1):
        engine.wait_ge(semaphore, count)


def graph_blocks(nc, x, adj, weight, w_ih, w_hh, b_ih, b_hh, att_w, att_a, out):
    graphs = x.shape[0]
    pairs = graphs // (2 * GROUP)
    assert x.shape[1:] == (P, D) and weight.shape[0] == LAYERS and graphs == pairs * 2 * GROUP

    ctx = ExitStack()
    with ctx:
        def sb(name, shape, dtype):
            return ctx.enter_context(nc.sbuf_tensor(name, shape, dtype))

        def sem(name):
            return ctx.enter_context(nc.semaphore(name))

        ident = sb("ident", [P, P], F32)
        wi_hi = sb("wi_hi", [P, LAYERS, KC, 3 * D], F32R)
        wi_lo = sb("wi_lo", [P, LAYERS, KC, 3 * D], F32R)
        wh_hi = sb("wh_hi", [P, KC, 3 * D], F32R)
        wh_lo = sb("wh_lo", [P, KC, 3 * D], F32R)
        wa_hi = sb("wa_hi", [P, KC, D], F32R)
        wa_lo = sb("wa_lo", [P, KC, D], F32R)
        c12 = sb("c12", [P, 2, D], F32)
        bih = sb("bih", [P, GATES], F32)
        bhh = sb("bhh", [P, GATES], F32)
        b_rz = sb("b_rz", [P, 4], F32)
        b_hn = sb("b_hn", [P, KC], F32)
        consts = sb("consts", [P, 4, GROUP], F32)
        quarter, per_d, eps, minus_half = (consts[:, i, :] for i in range(4))

        def both(name, shape, dtype):
            return [sb(f"{name}{a}", shape, dtype) for a in range(2)]

        x_in = both("x_in", [P, GROUP, D], F32)
        adj_in = both("adj_in", [P, GROUP, P], I32)
        adj_s = both("adj_s", [P, GROUP, P], F16)
        h_hi = both("h_hi", [P, KC, GROUP, P], F16)
        h_lo = both("h_lo", [P, KC, GROUP, P], F16)
        ht = both("ht", [P, KC, T], F32)
        ht_hi = [both(f"ht_hi{q}_", [P, KC, T], F32R) for q in range(2)]
        ht_lo = [both(f"ht_lo{q}_", [P, KC, T], F32R) for q in range(2)]
        nb_hi = both("nb_hi", [P, KC, T], F32R)
        nb_lo = both("nb_lo", [P, KC, T], F32R)
        relu_gnn = sb("relu_gnn", [P, GROUP, D], F32)

        def bank(name):
            return ctx.enter_context(nc.psum_tensor(name, [P, 512], F32))

        nb_bank, t_bank = bank("nb_bank"), bank("t_bank")
        KINDS = ("gnn", "att")
        stats = {k: sb(f"stats_{k}", [P, GROUP, 6], F32) for k in KINDS}
        ln_all = {k: sb(f"ln_{k}", [P, 11, GROUP], F32) for k in KINDS}
        ln = {k: [ln_all[k][:, i, :] for i in range(11)] for k in KINDS}
        x_in_loaded = [sem(f"x_in_loaded{a}") for a in range(2)]
        adj_in_loaded = [sem(f"adj_in_loaded{a}") for a in range(2)]
        relu_gnn_ready, first_h_hi_ready = sem("relu_gnn_ready"), sem("first_h_hi_ready")
        adj_s_ready, first_h_lo_ready = sem("adj_s_ready"), sem("first_h_lo_ready")
        stats_ready = {k: sem(f"stats_{k}_ready") for k in KINDS}
        ln_step = {k: sem(f"ln_step_{k}") for k in KINDS}
        LN_STEPS = 10
        first_ht_hi_ready, nb_hi_ready = sem("first_ht_hi_ready"), sem("nb_hi_ready")
        first_ht_lo_ready, nb_lo_ready = sem("first_ht_lo_ready"), sem("nb_lo_ready")
        h_lo_ready, x1_ready = sem("h_lo_ready"), sem("x1_ready")
        nb_done, first_t_done = sem("nb_done"), sem("first_t_done")

        x_v = x.rearrange("(n b) t d -> n t b d", b=GROUP)
        out_v = out.rearrange("(n b) t d -> n t b d", b=GROUP)
        adj_v = adj.rearrange("(n b) s t -> n s b t", b=GROUP)

        def dram_group(view, index):
            return view[bass.ds(index, 1)].rearrange("n t b d -> (n t) b d")

        def exists(p):
            return not isinstance(p, int) or 0 <= p < pairs

        def load_gnn(sp, p, a):
            index = sp.snap(p * 2 + a)
            wait_reached(sp, relu_gnn_ready, per_group(p - 1, a))
            sp.dma_start(x_in[a][:], dram_group(x_v, index)).then_inc(x_in_loaded[a], 16)
            wait_reached(sp, adj_s_ready, per_group(p - 1, a))
            sp.dma_start(adj_in[a][:], dram_group(adj_v, index)).then_inc(adj_in_loaded[a], 16)

        def statistics(kind, source):
            for b in range(GROUP):
                last = nc.vector.bn_stats(stats[kind][:, b, :], source[:, b, :])
            last.then_inc(stats_ready[kind], 1)

        def stats_gnn(dve, p, a):
            dve.wait_ge(x_in_loaded[a], per_load(p))
            wait_reached(dve, ln_step["gnn"], (per_group(p, a) - 1) * LN_STEPS)
            statistics("gnn", x_in[a])
            dve.wait_ge(adj_in_loaded[a], per_load(p))
            wait_reached(dve, nb_done, per_gate(p - 1, a, 2, 1))
            nc.vector.tensor_scalar(adj_s[a][:], adj_in[a][:], 0.0, 1.0 / HSCALE, ALU.not_equal,
                                    ALU.mult).then_inc(adj_s_ready, 1)

        def split_gnn(dve, p, a):
            dve.wait_ge(first_h_hi_ready, per_group(p, a))
            for c in range(KC):
                last = nc.vector.scalar_tensor_tensor(h_lo[a][:, c], relu_gnn[:, :, c * P:(c + 1) * P], HSCALE,
                                                      h_hi[a][:, c], ALU.mult, ALU.subtract)
            last.then_inc(first_h_lo_ready, 1)

        def norm(kind, source, target, ready):
            rstd, shift = ln[kind][7], ln[kind][9]
            for b in range(GROUP):
                last = nc.scalar.activation(target[:, b, :], source[:, b, :], ACT.Relu,
                                            bias=shift[:, b:b + 1], scale=rstd[:, b:b + 1])
            last.then_inc(ready, 1)

        def apply_gnn(act, p, a):
            wait_reached(act, first_t_done, per_chunk(p, a, 0) - 1)
            wait_reached(act, first_h_lo_ready, per_group(p, a) - 1)
            act.wait_ge(ln_step["gnn"], per_group(p, a) * LN_STEPS)
            norm("gnn", x_in[a], relu_gnn, relu_gnn_ready)
            wait_reached(act, nb_done, per_gate(p - 1, a, 2, 1))
            act.wait_ge(relu_gnn_ready, per_group(p, a))
            for c in range(KC):
                last = nc.scalar.activation(h_hi[a][:, c], relu_gnn[:, :, c * P:(c + 1) * P], ACT.Copy,
                                            scale=HSCALE)
            last.then_inc(first_h_hi_ready, 1)

        def norm_factors(pool, kind, p, a, last_read):
            base = (per_group(p, a) - 1) * LN_STEPS
            st = stats[kind]
            total, gap, m2, gap2, gap2_4, m2_d, var, rstd, scaled, shift, var_eps = ln[kind]
            step = ln_step[kind]
            pool.wait_ge(stats_ready[kind], per_group(p, a))
            wait_reached(pool, last_read, per_group(p, a) - 1)
            nc.gpsimd.tensor_tensor(total, st[:, :, 1], st[:, :, 4], ALU.add).then_inc(step, 1)
            nc.gpsimd.tensor_tensor(gap, st[:, :, 1], st[:, :, 4], ALU.subtract).then_inc(step, 1)
            nc.gpsimd.tensor_tensor(m2, st[:, :, 2], st[:, :, 5], ALU.add).then_inc(step, 1)
            pool.wait_ge(step, base + 2)
            nc.gpsimd.tensor_tensor(scaled, total, minus_half, ALU.mult)
            nc.gpsimd.tensor_tensor(gap2, gap, gap, ALU.mult).then_inc(step, 1)
            pool.wait_ge(step, base + 3)
            nc.gpsimd.tensor_tensor(m2_d, m2, per_d, ALU.mult).then_inc(step, 1)
            pool.wait_ge(step, base + 4)
            nc.gpsimd.tensor_tensor(gap2_4, gap2, quarter, ALU.mult).then_inc(step, 1)
            pool.wait_ge(step, base + 6)
            nc.gpsimd.tensor_tensor(var, gap2_4, m2_d, ALU.add).then_inc(step, 1)
            pool.wait_ge(step, base + 7)
            nc.gpsimd.tensor_tensor(var_eps, var, eps, ALU.add).then_inc(step, 1)
            pool.wait_ge(step, base + 8)
            nc.gpsimd.tensor_tensor(rstd, var_eps, minus_half, ALU.pow).then_inc(step, 1)
            pool.wait_ge(step, base + 9)
            nc.gpsimd.tensor_tensor(shift, scaled, rstd, ALU.mult).then_inc(step, 1)

        def products(bank_ap, terms, start=True, stop=True):
            todo = [m for w_hi, w_lo, d_hi, d_lo in terms for m in ((w_hi, d_hi), (w_hi, d_lo), (w_lo, d_hi))]
            for i, (w, d) in enumerate(todo):
                last = nc.tensor.matmul(bank_ap, w, d, start=start and i == 0,
                                        stop=stop and i == len(todo) - 1)
            return last

        def group_transposes(source, blocks):
            for b in range(GROUP):
                last = nc.tensor.transpose(t_bank[:, b * P:(b + 1) * P], blocks(source, b), ident[:])
            return last

        def first_transpose_pe(pe, p, a, c):
            pe.wait_ge(relu_gnn_ready, per_group(p, a))
            wait_reached(pe, first_ht_lo_ready, per_chunk(p, a, c) - 1)
            wait_reached(pe, x1_ready, per_chunk(p - 1, a, c))
            group_transposes(relu_gnn, lambda s, b: s[:, b, c * P:(c + 1) * P]).then_inc(first_t_done, 1)

        def neighbours_pe(pe, p, a, layer, c):
            n = per_gate(p, a, layer, c)
            if layer == 0:
                pe.wait_ge(first_h_lo_ready, per_group(p, a))
                pe.wait_ge(adj_s_ready, per_group(p, a))
            else:
                pe.wait_ge(h_lo_ready, per_later_layer(p, a, layer, c))
            wait_reached(pe, nb_lo_ready, n - 1)
            for b in range(GROUP):
                block_ap = nb_bank[:, b * P:(b + 1) * P]
                nc.tensor.matmul(block_ap, h_hi[a][:, c, b, :], adj_s[a][:, b, :], start=True, stop=False)
                last = nc.tensor.matmul(block_ap, h_lo[a][:, c, b, :], adj_s[a][:, b, :],
                                        start=False, stop=True)
            last.then_inc(nb_done, 1)

        def first_transpose_act(act, p, a, c):
            act.wait_ge(first_t_done, per_chunk(p, a, c))
            nc.scalar.activation(ht[a][:, c, :], t_bank[:], ACT.Copy)
            nc.scalar.activation(ht_hi[0][a][:, c, :], t_bank[:], ACT.Copy).then_inc(first_ht_hi_ready, 1)

        def neighbours_act(act, p, a, layer, c):
            act.wait_ge(nb_done, per_gate(p, a, layer, c))
            nc.scalar.activation(nb_hi[a][:, c, :], nb_bank[:], ACT.Copy).then_inc(nb_hi_ready, 1)

        def low_part(lo, whole, hi, ready):
            nc.vector.tensor_tensor(lo, whole, hi.bitcast(F32), ALU.subtract).then_inc(ready, 1)

        def first_transpose_dve(dve, p, a, c):
            dve.wait_ge(first_ht_hi_ready, per_chunk(p, a, c))
            low_part(ht_lo[0][a][:, c, :], t_bank[:], ht_hi[0][a][:, c, :], first_ht_lo_ready)

        def neighbours_dve(dve, p, a, layer, c):
            dve.wait_ge(nb_hi_ready, per_gate(p, a, layer, c))
            low_part(nb_lo[a][:, c, :], nb_bank[:], nb_hi[a][:, c, :], nb_lo_ready)

        with ExitStack() as setup:
            def tmp(name, shape, dtype=F32):
                return setup.enter_context(nc.sbuf_tensor(name, shape, dtype))

            raw_ih = tmp("raw_ih", [P, GATES, D])
            raw_hh = tmp("raw_hh", [P, GATES, D])
            raw_w = tmp("raw_w", [P, LAYERS, KC, D])
            raw_att = tmp("raw_att", [P, KC, D])
            att_col = tmp("att_col", [P, 2, KC])
            ih_hi = tmp("ih_hi", [P, KC, 3 * D], F32R)
            ih_lo = tmp("ih_lo", [P, KC, 3 * D], F32R)
            w_hi = tmp("w_hi", [P, LAYERS, KC, D], F32R)
            w_lo = tmp("w_lo", [P, LAYERS, KC, D], F32R)
            banks = [setup.enter_context(nc.psum_tensor(f"setup_bank{i}", [P, 512], F32)) for i in range(6)]
            LOADS = ("ih", "ih_tail", "w", "hh", "att", "col", "bih", "bhh")
            loaded = {what: setup.enter_context(nc.semaphore(f"{what}_loaded")) for what in LOADS}
            ident_ready = setup.enter_context(nc.semaphore("ident_ready"))
            bank_full = setup.enter_context(nc.semaphore("bank_full"))
            hi_ready = setup.enter_context(nc.semaphore("hi_ready"))
            bank_read = setup.enter_context(nc.semaphore("bank_read"))
            bias_step = setup.enter_context(nc.semaphore("bias_step"))

            COLS = (slice(0, 2 * D), slice(2 * D, 3 * D))
            HALF = (slice(0, 3 * P), slice(3 * P, 6 * P))
            fills = [("ih", k, half) for half in range(2) for k in range(KC)]
            fills += [("w", (layer, k), 0) for layer in range(LAYERS) for k in range(KC)]
            transposed = len(fills)
            fills += [("wi", (0, k), part) for k in range(KC) for part in range(2)]
            fills += [("wi", (1, k), part) for k in range(KC) for part in range(2)]
            fills += [("hh", k, part) for k in range(KC) for part in range(2)]
            fills += [("wi", (2, k), part) for k in range(KC) for part in range(2)]
            fills += [("att", k, 0) for k in range(KC)] + [("col", 0, 0)]

            def setup_order(fill, side):
                for n, (what, where, which) in enumerate(fills):
                    fill(n, what, where, which)
                    for stage, *group in SETUP_SIDE.get(n, ()):
                        if stage in side:
                            side[stage](0, *group)

            def split_target(what, where, which):
                if what == "ih":
                    return ih_hi[:, where, HALF[which]], ih_lo[:, where, HALF[which]], 1.0
                if what == "w":
                    layer, e = where
                    return w_hi[:, layer, e, :], w_lo[:, layer, e, :], 1.0
                if what == "hh":
                    return wh_hi[:, where, COLS[which]], wh_lo[:, where, COLS[which]], (0.5 if which else 1.0)
                if what == "att":
                    return wa_hi[:, where, :], wa_lo[:, where, :], 1.0
                if what == "col":
                    return c12[:, 0, :], c12[:, 1, :], 1.0
                layer, k = where
                return wi_hi[:, layer, k, COLS[which]], wi_lo[:, layer, k, COLS[which]], 1.0

            with nc.Block() as block:
                @block.sync
                def _(sp):
                    ih_v = w_ih.rearrange("(c p) e -> p c e", p=P)
                    for half in range(2):
                        sp.dma_start(raw_ih[:, 3 * half:3 * half + 3], ih_v[:, 3 * half:3 * half + 3]).then_inc(
                            loaded["ih_tail" if half else "ih"], 16)
                    sp.dma_start(raw_w[:], weight.rearrange("l (c p) e -> p l c e", p=P)).then_inc(loaded["w"], 16)
                    load_gnn(sp, 0, 0)
                    sp.dma_start(raw_hh[:], w_hh.rearrange("(c p) e -> p c e", p=P)).then_inc(loaded["hh"], 16)
                    load_gnn(sp, 0, 1)
                    sp.dma_start(raw_att[:], att_w.rearrange("(c p) f -> p c f", p=P)).then_inc(loaded["att"], 16)
                    with nc.allow_non_contiguous_dma(reason="small vectors, once"):
                        sp.dma_start(att_col[:], att_a.rearrange("o (w k p) -> p (o w) k", w=2, p=P)).then_inc(
                            loaded["col"], 16)
                        sp.dma_start(bih[:], b_ih.rearrange("(c p) -> p c", p=P)).then_inc(loaded["bih"], 16)
                        sp.dma_start(bhh[:], b_hh.rearrange("(c p) -> p c", p=P)).then_inc(loaded["bhh"], 16)

                @block.gpsimd
                def _(pool):
                    nc.gpsimd.memset(ident[:], 0.0).then_inc(ident_ready, 1)
                    nc.gpsimd.memset(quarter, 0.25)
                    nc.gpsimd.memset(per_d, 1.0 / D)
                    nc.gpsimd.memset(eps, EPS)
                    nc.gpsimd.memset(minus_half, -0.5).then_inc(ident_ready, 1)
                    pool.wait_ge(ident_ready, 2)
                    nc.gpsimd.affine_select(out=ident[:], in_=ident[:], compare_op=ALU.not_equal, fill=1.0, base=0,
                                            pattern=[[-1, P]], channel_multiplier=1).then_inc(ident_ready, 1)
                    setup_order(lambda *fill: None, {
                        "stats_gnn": lambda p, a: norm_factors(pool, "gnn", p, a, relu_gnn_ready)})

                @block.tensor
                def _(pe):
                    def fill(n, what, where, which):
                        bank = banks[n % len(banks)]
                        if what != "wi":
                            pe.wait_ge(loaded["ih_tail" if what == "ih" and which else what], 16)
                        if n >= len(banks):
                            pe.wait_ge(bank_read, n + 1 - len(banks))
                        if what == "ih":
                            for j in range(3):
                                last = nc.tensor.transpose(bank[:, j * P:(j + 1) * P],
                                                           raw_ih[:, 3 * which + j, where * P:(where + 1) * P], ident[:])
                        elif what == "w":
                            layer, e = where
                            for j in range(KC):
                                last = nc.tensor.transpose(bank[:, j * P:(j + 1) * P],
                                                           raw_w[:, layer, j, e * P:(e + 1) * P], ident[:])
                        elif what == "hh":
                            for j in range(4 if which == 0 else 2):
                                last = nc.tensor.transpose(bank[:, j * P:(j + 1) * P],
                                                           raw_hh[:, 4 * which + j, where * P:(where + 1) * P], ident[:])
                        elif what == "att":
                            for j in range(KC):
                                last = nc.tensor.transpose(bank[:, j * P:(j + 1) * P],
                                                           raw_att[:, j, where * P:(where + 1) * P], ident[:])
                        elif what == "col":
                            for i in range(2):
                                for j in range(KC):
                                    last = nc.tensor.matmul(bank[:, i * D:(i + 1) * D],
                                                            att_col[:, i, j:j + 1].broadcast_to([P, P]),
                                                            raw_att[:, j, :], start=(j == 0), stop=(j == KC - 1))
                        else:
                            layer, k = where
                            cols = COLS[which]
                            pe.wait_ge(bank_read, transposed)
                            last = products(bank[:, 0:cols.stop - cols.start],
                                            [(w_hi[:, layer, e, k * P:(k + 1) * P], w_lo[:, layer, e, k * P:(k + 1) * P],
                                              ih_hi[:, e, cols], ih_lo[:, e, cols]) for e in range(KC)])
                        last.then_inc(bank_full, 1)

                    pe.wait_ge(ident_ready, 3)
                    setup_order(fill, {"first_transpose": lambda *which: first_transpose_pe(pe, *which),
                                       "neighbours": lambda p, a, c: neighbours_pe(pe, p, a, 0, c)})

                @block.scalar
                def _(act):
                    def fill(n, *which):
                        hi, _, scale = split_target(*which)
                        act.wait_ge(bank_full, n + 1)
                        nc.scalar.activation(hi, banks[n % len(banks)][:, 0:hi.shape[-1]], ACT.Copy,
                                             scale=scale).then_inc(hi_ready, 1)

                    setup_order(fill, {"apply_gnn": lambda p, a: apply_gnn(act, p, a),
                                       "first_transpose": lambda *which: first_transpose_act(act, *which),
                                       "neighbours": lambda p, a, c: neighbours_act(act, p, a, 0, c)})

                @block.vector
                def _(dve):
                    def fill(n, *which):
                        hi, lo, scale = split_target(*which)
                        dve.wait_ge(hi_ready, n + 1)
                        if which[0] == "col":
                            nc.vector.tensor_copy(lo, banks[n % len(banks)][:, D:2 * D]).then_inc(bank_read, 1)
                            return
                        nc.vector.scalar_tensor_tensor(lo, banks[n % len(banks)][:, 0:lo.shape[-1]], scale,
                                                       hi.bitcast(F32), ALU.mult, ALU.subtract).then_inc(bank_read, 1)

                    setup_order(fill, {"stats_gnn": lambda p, a: stats_gnn(dve, p, a),
                                       "split_gnn": lambda p, a: split_gnn(dve, p, a),
                                       "first_transpose": lambda *which: first_transpose_dve(dve, *which),
                                       "neighbours": lambda p, a, c: neighbours_dve(dve, p, a, 0, c)})
                    for what in ("bih", "bhh"):
                        dve.wait_ge(loaded[what], 16)
                    nc.vector.tensor_tensor(b_rz[:], bih[:, 0:4], bhh[:, 0:4], ALU.add).then_inc(bias_step, 1)
                    dve.wait_ge(bias_step, 1)
                    nc.vector.tensor_scalar(b_rz[:], b_rz[:], 0.5, None, ALU.mult)
                    nc.vector.tensor_scalar(b_hn[:], bhh[:, 4:6], 0.5, None, ALU.mult)

        x_res = both("x_res", [P, GROUP, D], F32)
        adj_att = both("adj_att", [P, GROUP, P], I32)
        u_hi = both("u_hi", [P, GROUP, D], F16)
        u_lo = both("u_lo", [P, GROUP, D], F16)
        s12 = both("s12", [P, GROUP, 2], F32)
        row_scale = both("row_scale", [P, GROUP], F32)
        relu_att = sb("relu_att", [P, GROUP, D], F32)
        dot_terms = sb("dot_terms", [P, GROUP, 2, D], F32)
        vt_hi = sb("vt_hi", [P, KC, T], F32R)
        vt_lo = sb("vt_lo", [P, KC, T], F32R)
        hn_b = [sb(f"hn_b{c}", [P, T], F32) for c in range(2)]
        tanh_r = [sb(f"tanh_r{c}", [P, T], F32) for c in range(2)]
        tanh_z = [sb(f"tanh_z{c}", [P, T], F32) for c in range(2)]
        n_pre = [sb(f"n_pre{c}", [P, T], F32) for c in range(2)]
        n_out = [sb(f"n_out{c}", [P, T], F32) for c in range(2)]
        diff = [sb(f"diff{c}", [P, T], F32) for c in range(2)]
        score = sb("score", [P, GROUP, P], F32)
        prob = sb("prob", [P, GROUP, P], F32)
        pt_hi = sb("pt_hi", [P, GROUP, P], F16)
        pt_lo = sb("pt_lo", [P, GROUP, P], F16)
        row_max = sb("row_max", [P, GROUP], F32)
        minus_max = sb("minus_max", [P, GROUP], F32)
        row_sum = sb("row_sum", [P, GROUP], F32)
        row_inv = sb("row_inv", [P, GROUP], F32)

        hn_bank, r_bank, in_bank, z_bank = bank("hn_bank"), bank("r_bank"), bank("in_bank"), bank("z_bank")
        w_bank, s_bank = bank("w_bank"), bank("s_bank")

        def after_gates(p):
            return isinstance(p, int) and p == pairs - 1

        def scores_bank(p, a):
            return hn_bank if after_gates(p) and a == 1 else s_bank

        def gather_bank(p, half):
            return r_bank if after_gates(p) and half == 1 else s_bank

        def attend_bank(p, half):
            return (z_bank, nb_bank)[half] if after_gates(p) else w_bank

        x_res_loaded = [sem(f"x_res_loaded{a}") for a in range(2)]
        adj_att_loaded = [sem(f"adj_att_loaded{a}") for a in range(2)]
        out_stored = [sem(f"out_stored{a}") for a in range(2)]
        hn_done, r_done, in_done, z_done = sem("hn_done"), sem("r_done"), sem("in_done"), sem("z_done")
        t_done, res_t_done = sem("t_done"), sem("res_t_done")
        gather_done, s2_done, probs_t_done, attend_done = (sem("gather_done"), sem("s2_done"), sem("probs_t_done"),
                                                       sem("attend_done"))
        hn_ready, tanh_r_ready, n_ready, tanh_z_ready = (sem("hn_ready"), sem("tanh_r_ready"), sem("n_ready"),
                                                         sem("tanh_z_ready"))
        ht_hi_ready = sem("ht_hi_ready")
        h_hi_ready = sem("h_hi_ready")
        relu_att_ready = sem("relu_att_ready")
        u_hi_ready, vt_hi_ready, prob_ready, pt_hi_ready = (sem("u_hi_ready"), sem("vt_hi_ready"),
                                                             sem("prob_ready"), sem("pt_hi_ready"))
        rn_ready, n_pre_ready, diff_ready, zdiff_ready, h_ready = (sem("rn_ready"), sem("n_pre_ready"),
                                                                   sem("diff_ready"), sem("zdiff_ready"),
                                                                   sem("h_ready"))
        ht_lo_ready = sem("ht_lo_ready")
        u_lo_ready, vt_lo_ready, pt_lo_ready = sem("u_lo_ready"), sem("vt_lo_ready"), sem("pt_lo_ready")
        dots_ready = sem("dots_ready")
        mask_ready, sum_ready, leaky_ready, masked_ready, max_ready, minus_max_ready = (
            sem("mask_ready"), sem("sum_ready"), sem("leaky_ready"), sem("masked_ready"), sem("max_ready"),
            sem("minus_max_ready"))
        inv_ready, row_scale_ready, out_ready = sem("inv_ready"), sem("row_scale_ready"), sem("out_ready")

        def slots(p, gate, side):
            for slot in range(2 * LAYERS):
                for step in range(len(STEPS)):
                    gate(p, slot % 2, slot // 2, STEPS[step][:-1], step // 4)
                    last_slot = slot == 2 * LAYERS - 1 and not exists(p + 1)
                    for stage, *which, offset in (LAST_SLOT_SIDE if last_slot else SIDE).get((slot, step), ()):
                        if stage in side and exists(p + offset):
                            side[stage](p + offset, *which)

        def all_pairs(engine, gate, side):
            for stage, *which in HEAD:
                if stage in side:
                    side[stage](0, *which)
            slots(0, gate, side)
            with engine.Fori(1, pairs - 1) as p:
                slots(p, gate, side)
            slots(pairs - 1, gate, side)
            for stage, *which in TAIL:
                if stage in side:
                    side[stage](pairs - 1, *which)

        with nc.Block() as block:
            @block.sync
            def _(sp):
                def store(p, a):
                    index = sp.snap(p * 2 + a)
                    sp.wait_ge(out_ready, per_chunk(p, a, 1))
                    sp.dma_start(dram_group(out_v, index), x_res[a][:]).then_inc(out_stored[a], 16)

                def load_att(p, a):
                    index = sp.snap(p * 2 + a)
                    wait_reached(sp, out_stored[a], per_load(p - 1))
                    sp.dma_start(x_res[a][:], dram_group(x_v, index)).then_inc(x_res_loaded[a], 16)
                    wait_reached(sp, mask_ready, per_group(p - 1, a))
                    sp.dma_start(adj_att[a][:], dram_group(adj_v, index)).then_inc(adj_att_loaded[a], 16)

                def pair(p):
                    for a in range(2):
                        if exists(p + 1):
                            load_gnn(sp, p + 1, a)
                    for a in range(2):
                        if exists(p - 1):
                            store(p - 1, a)
                        load_att(p, a)

                pair(0)
                with sp.Fori(1, pairs - 1) as p:
                    pair(p)
                pair(pairs - 1)
                for a in range(2):
                    store(pairs - 1, a)
                for a in range(2):
                    sp.wait_ge(out_stored[a], per_load(pairs - 1))

            @block.tensor
            def _(pe):

                def gate(p, a, layer, name, c):
                    n = per_gate(p, a, layer, c)
                    row = {"hn": 4, "r": 0, "in": 4, "z": 2}[name] + c
                    cols = slice(row * P, (row + 1) * P)
                    from_h = [(wh_hi[:, k, cols], wh_lo[:, k, cols], ht_hi[layer % 2][a][:, k, :],
                               ht_lo[layer % 2][a][:, k, :]) for k in range(KC)]
                    from_nb = [(wi_hi[:, layer, k, cols], wi_lo[:, layer, k, cols], nb_hi[a][:, k, :],
                                nb_lo[a][:, k, :]) for k in range(KC)]
                    if name == "hn":
                        if c == 0 and layer == 0:
                            pe.wait_ge(first_ht_lo_ready, per_chunk(p, a, 1))
                        elif c == 0:
                            pe.wait_ge(ht_lo_ready, per_later_layer(p, a, layer, 1))
                        wait_reached(pe, hn_ready, n - 1)
                        products(hn_bank[:], from_h).then_inc(hn_done, 1)
                    elif name == "r":
                        wait_reached(pe, tanh_r_ready, n - 1)
                        products(r_bank[:], from_h, stop=False)
                        if c == 0:
                            pe.wait_ge(nb_lo_ready, per_gate(p, a, layer, 1))
                        products(r_bank[:], from_nb, start=False).then_inc(r_done, 1)
                    elif name == "in":
                        wait_reached(pe, n_pre_ready, n - 1)
                        products(in_bank[:], from_nb).then_inc(in_done, 1)
                    else:
                        wait_reached(pe, tanh_z_ready, n - 1)
                        products(z_bank[:], from_h + from_nb).then_inc(z_done, 1)

                def columns_of(source, b):
                    return source[:, b * P:(b + 1) * P]

                def transpose(p, a, layer, c):
                    pe.wait_ge(h_ready, per_gate(p, a, layer - 1, c))
                    wait_reached(pe, h_lo_ready, per_later_layer(p, a, layer, c) - 1)
                    if layer == 1 and a == 0 and c == 0:
                        pe.wait_ge(first_ht_lo_ready, per_chunk(p, 1, 1))
                    group_transposes(ht[a][:, c, :], columns_of).then_inc(t_done, 1)

                def residual(p, a, c):
                    pe.wait_ge(h_ready, per_gate(p, a, LAYERS - 1, c))
                    wait_reached(pe, x1_ready, per_chunk(p, a, c) - 1)
                    if a == 0 and c == 0:
                        pe.wait_ge(h_lo_ready, per_later_layer(p, 1, 2, 1))
                    if exists(p + 1) and (a, c) != (0, 0):
                        before = (0, 0) if a == 0 else ((0, 1) if c == 0 else (1, 0))
                        pe.wait_ge(first_ht_lo_ready, per_chunk(p + 1, *before))
                    group_transposes(ht[a][:, c, :], columns_of).then_inc(res_t_done, 1)

                def scores(p, a):
                    pe.wait_ge(dots_ready, per_group(p, a))
                    if after_gates(p) and a == 1:
                        pe.wait_ge(hn_ready, per_gate(p, 1, LAYERS - 1, 1))
                    else:
                        wait_reached(pe, vt_lo_ready, per_chunk(p, a, 0) - 1)
                    for b in range(GROUP):
                        last = nc.tensor.transpose(scores_bank(p, a)[:, b * P:(b + 1) * P],
                                                   s12[a][:, b, 1:2].broadcast_to([P, P]), ident[:])
                    last.then_inc(s2_done, 1)

                def probs_transpose(p, a):
                    pe.wait_ge(prob_ready, per_group(p, a))
                    for b in range(GROUP):
                        last = nc.tensor.transpose(s_bank[:, b * P:(b + 1) * P], prob[:, b, :], ident[:])
                    last.then_inc(probs_t_done, 1)

                def gather(p, a, half):
                    n = per_chunk(p, a, half)
                    pe.wait_ge(u_lo_ready, per_group(p, a))
                    pe.wait_ge(pt_lo_ready, per_group(p, a))
                    if after_gates(p) and half == 1:
                        pe.wait_ge(tanh_r_ready, per_gate(p, 1, LAYERS - 1, 1))
                        if a == 1:
                            pe.wait_ge(vt_lo_ready, n - 2)
                    elif half == 1:
                        pe.wait_ge(vt_lo_ready, n - 1)
                    for k in range(KC):
                        for i in range(2):
                            b = 2 * half + i
                            target = gather_bank(p, half)[:, (2 * k + i) * P:(2 * k + i + 1) * P]
                            cols = slice(k * P, (k + 1) * P)
                            last = products(target, [(u_hi[a][:, b, cols], u_lo[a][:, b, cols],
                                                      pt_hi[:, b, :], pt_lo[:, b, :])])
                    last.then_inc(gather_done, 1)

                def attend(p, a, half):
                    n = per_chunk(p, a, half)
                    pe.wait_ge(vt_lo_ready, n)
                    if after_gates(p) and a == 0:
                        pe.wait_ge(tanh_z_ready, per_gate(p, 1, LAYERS - 1, 1))
                        pe.wait_ge(nb_lo_ready, per_gate(p, 1, LAYERS - 1, 1))
                    else:
                        wait_reached(pe, out_ready, n - 2 if after_gates(p) else n - 1)
                    for i in range(2):
                        nodes = slice((2 * half + i) * P, (2 * half + i + 1) * P)
                        last = products(attend_bank(p, half)[:, i * D:(i + 1) * D],
                                        [(vt_hi[:, k, nodes], vt_lo[:, k, nodes], wa_hi[:, k, :], wa_lo[:, k, :])
                                         for k in range(KC)])
                    last.then_inc(attend_done, 1)

                all_pairs(pe, gate, {
                    "first_transpose": lambda *which: first_transpose_pe(pe, *which), "transpose": transpose,
                    "residual": residual, "neighbours": lambda *which: neighbours_pe(pe, *which), "gather": gather,
                    "scores": scores, "probs_transpose": probs_transpose, "attend": attend})

            @block.scalar
            def _(act):
                def gate(p, a, layer, name, c):
                    n = per_gate(p, a, layer, c)
                    if name == "hn":
                        act.wait_ge(hn_done, n)
                        wait_reached(act, rn_ready, n - 2)
                        nc.scalar.activation(hn_b[c][:], hn_bank[:], ACT.Identity,
                                             bias=b_hn[:, c:c + 1]).then_inc(hn_ready, 1)
                    elif name == "r":
                        act.wait_ge(r_done, n)
                        wait_reached(act, rn_ready, n - 2)
                        nc.scalar.activation(tanh_r[c][:], r_bank[:], ACT.Tanh, bias=b_rz[:, c:c + 1],
                                             scale=0.5).then_inc(tanh_r_ready, 1)
                    elif name == "z":
                        act.wait_ge(n_pre_ready, n)
                        wait_reached(act, h_ready, n - 2)
                        nc.scalar.activation(n_out[c][:], n_pre[c][:], ACT.Tanh,
                                             bias=bih[:, 4 + c:5 + c]).then_inc(n_ready, 1)
                        act.wait_ge(z_done, n)
                        wait_reached(act, zdiff_ready, n - 2)
                        nc.scalar.activation(tanh_z[c][:], z_bank[:], ACT.Tanh, bias=b_rz[:, 2 + c:3 + c],
                                             scale=0.5).then_inc(tanh_z_ready, 1)

                def split_state(p, a, layer, c):
                    act.wait_ge(h_ready, per_gate(p, a, layer - 1, c))
                    nc.scalar.activation(ht_hi[layer % 2][a][:, c, :], ht[a][:, c, :],
                                         ACT.Copy).then_inc(ht_hi_ready, 1)

                def apply_att(p, a):
                    wait_reached(act, u_lo_ready, per_group(p, a) - 1)
                    wait_reached(act, dots_ready, per_group(p, a) - 1)
                    act.wait_ge(ln_step["att"], per_group(p, a) * LN_STEPS)
                    norm("att", x_res[a], relu_att, relu_att_ready)

                def split_att(p, a):
                    wait_reached(act, gather_done, per_chunk(p, 0, 0) - 1)
                    act.wait_ge(relu_att_ready, per_group(p, a))
                    nc.scalar.activation(u_hi[a][:], relu_att[:], ACT.Copy, scale=HSCALE).then_inc(u_hi_ready, 1)

                def transpose(p, a, layer, c):
                    act.wait_ge(t_done, per_later_layer(p, a, layer, c))
                    nc.scalar.activation(h_hi[a][:, c].rearrange("p b t -> p (b t)"), t_bank[:], ACT.Copy,
                                         scale=HSCALE).then_inc(h_hi_ready, 1)

                def softmax(p, a):
                    act.wait_ge(minus_max_ready, per_group(p, a))
                    wait_reached(act, probs_t_done, per_group(p, a) - 1)
                    for b in range(GROUP):
                        last = nc.scalar.activation(prob[:, b, :], score[:, b, :], ACT.Exp,
                                                    bias=minus_max[:, b:b + 1], accum_out=row_sum[:, b:b + 1])
                    last.then_inc(prob_ready, 1)

                def probs_transpose(p, a):
                    act.wait_ge(probs_t_done, per_group(p, a))
                    wait_reached(act, gather_done, per_chunk(p, a, 0) - 1)
                    nc.scalar.activation(pt_hi[:].rearrange("p b t -> p (b t)"), s_bank[:], ACT.Copy,
                                         scale=PSCALE).then_inc(pt_hi_ready, 1)

                def gather(p, a, half):
                    act.wait_ge(gather_done, per_chunk(p, a, half))
                    wait_reached(act, attend_done, per_chunk(p, a, 0) - 1)
                    nc.scalar.activation(vt_hi[:, :, 2 * P * half:2 * P * (half + 1)],
                                         gather_bank(p, half)[:].rearrange("p (k t) -> p k t", k=KC), ACT.Copy,
                                         scale=1.0 / (HSCALE * PSCALE)).then_inc(vt_hi_ready, 1)

                all_pairs(act, gate, {
                    "apply_gnn": lambda p, a: apply_gnn(act, p, a), "apply_att": apply_att, "split_state": split_state,
                    "first_transpose": lambda *which: first_transpose_act(act, *which), "transpose": transpose,
                    "neighbours": lambda *which: neighbours_act(act, *which), "split_att": split_att,
                    "gather": gather, "softmax": softmax,
                    "probs_transpose": probs_transpose})

            @block.vector
            def _(dve):
                def gate(p, a, layer, name, c):
                    n = per_gate(p, a, layer, c)
                    if name == "r":
                        dve.wait_ge(hn_ready, n)
                        dve.wait_ge(tanh_r_ready, n)
                        wait_reached(dve, n_ready, n - 2)
                        nc.vector.scalar_tensor_tensor(n_pre[c][:], tanh_r[c][:], 1.0, hn_b[c][:], ALU.add,
                                                       ALU.mult).then_inc(rn_ready, 1)
                    elif name == "in":
                        dve.wait_ge(rn_ready, n)
                        dve.wait_ge(in_done, n)
                        nc.vector.tensor_tensor(n_pre[c][:], n_pre[c][:], in_bank[:], ALU.add).then_inc(n_pre_ready, 1)

                def update(p, a, layer, c):
                    n = per_gate(p, a, layer, c)
                    dve.wait_ge(n_ready, n)
                    wait_reached(dve, h_ready, n - 2)
                    nc.vector.tensor_tensor(diff[c][:], ht[a][:, c, :], n_out[c][:], ALU.subtract).then_inc(diff_ready, 1)
                    dve.wait_ge(diff_ready, n)
                    dve.wait_ge(tanh_z_ready, n)
                    nc.vector.scalar_tensor_tensor(diff[c][:], tanh_z[c][:], 1.0, diff[c][:], ALU.add,
                                                   ALU.mult).then_inc(zdiff_ready, 1)
                    dve.wait_ge(zdiff_ready, n)
                    nc.vector.scalar_tensor_tensor(ht[a][:, c, :], diff[c][:], 0.5, n_out[c][:], ALU.mult,
                                                   ALU.add).then_inc(h_ready, 1)

                def split_state(p, a, layer, c):
                    q = layer % 2
                    dve.wait_ge(ht_hi_ready, per_later_layer(p, a, layer, c))
                    low_part(ht_lo[q][a][:, c, :], ht[a][:, c, :], ht_hi[q][a][:, c, :], ht_lo_ready)

                def stats_att(p, a):
                    dve.wait_ge(x1_ready, per_chunk(p, a, 1))
                    wait_reached(dve, ln_step["att"], (per_group(p, a) - 1) * LN_STEPS)
                    statistics("att", x_res[a])

                def transpose(p, a, layer, c):
                    dve.wait_ge(h_hi_ready, per_later_layer(p, a, layer, c))
                    nc.vector.scalar_tensor_tensor(h_lo[a][:, c].rearrange("p b t -> p (b t)"), t_bank[:], HSCALE,
                                                   h_hi[a][:, c].rearrange("p b t -> p (b t)"), ALU.mult,
                                                   ALU.subtract).then_inc(h_lo_ready, 1)

                def residual(p, a, c):
                    dve.wait_ge(x_res_loaded[a], per_load(p))
                    dve.wait_ge(res_t_done, per_chunk(p, a, c))
                    part = x_res[a][:, :, c * P:(c + 1) * P]
                    nc.vector.tensor_tensor(part, part, t_bank[:].rearrange("p (b t) -> p b t", b=GROUP),
                                            ALU.add).then_inc(x1_ready, 1)

                def split_att(p, a):
                    dve.wait_ge(u_hi_ready, per_group(p, a))
                    wait_reached(dve, gather_done, per_chunk(p, 0, 0) - 1)
                    nc.vector.scalar_tensor_tensor(u_lo[a][:], relu_att[:], HSCALE, u_hi[a][:], ALU.mult,
                                                   ALU.subtract).then_inc(u_lo_ready, 1)

                def dots(p, a, half):
                    for b in (2 * half, 2 * half + 1):
                        for i in range(2):
                            last = nc.vector.tensor_tensor_reduce(dot_terms[:, b, i, :], relu_att[:, b, :],
                                                                  c12[:, i, :], 1.0, 0.0, ALU.mult, ALU.add,
                                                                  s12[a][:, b, i:i + 1])
                    if half == 1:
                        last.then_inc(dots_ready, 1)

                def scores(p, a):
                    n = per_group(p, a)
                    dve.wait_ge(adj_att_loaded[a], per_load(p))
                    wait_reached(dve, probs_t_done, n - 1)
                    nc.vector.tensor_scalar(prob[:], adj_att[a][:], 0.0, MASKED, ALU.is_equal,
                                            ALU.mult).then_inc(mask_ready, 1)
                    dve.wait_ge(s2_done, n)
                    wait_reached(dve, prob_ready, n - 1)
                    nc.vector.tensor_tensor(score[:], scores_bank(p, a)[:].rearrange("p (b t) -> p b t", b=GROUP),
                                            s12[a][:, :, 0:1].broadcast_to([P, GROUP, P]),
                                            ALU.add).then_inc(sum_ready, 1)
                    dve.wait_ge(sum_ready, n)
                    nc.vector.scalar_tensor_tensor(score[:], score[:], ALPHA, score[:], ALU.mult,
                                                   ALU.max).then_inc(leaky_ready, 1)
                    dve.wait_ge(leaky_ready, n)
                    dve.wait_ge(mask_ready, n)
                    nc.vector.tensor_tensor(score[:], score[:], prob[:], ALU.add).then_inc(masked_ready, 1)
                    dve.wait_ge(masked_ready, n)
                    nc.vector.tensor_reduce(row_max[:], score[:], AX_X, ALU.max).then_inc(max_ready, 1)
                    dve.wait_ge(max_ready, n)
                    nc.vector.tensor_scalar(minus_max[:], row_max[:], -1.0, None, ALU.mult).then_inc(minus_max_ready, 1)

                def probs_transpose(p, a):
                    n = per_group(p, a)
                    dve.wait_ge(prob_ready, n)
                    nc.vector.reciprocal(row_inv[:], row_sum[:]).then_inc(inv_ready, 1)
                    dve.wait_ge(inv_ready, n)
                    nc.vector.scalar_tensor_tensor(row_scale[a][:], row_max[:], 0.5 * MASKED, row_inv[:], ALU.is_gt,
                                                   ALU.mult).then_inc(row_scale_ready, 1)
                    dve.wait_ge(pt_hi_ready, n)
                    nc.vector.scalar_tensor_tensor(pt_lo[:].rearrange("p b t -> p (b t)"), s_bank[:], PSCALE,
                                                   pt_hi[:].rearrange("p b t -> p (b t)"), ALU.mult,
                                                   ALU.subtract).then_inc(pt_lo_ready, 1)

                def gather(p, a, half):
                    dve.wait_ge(vt_hi_ready, per_chunk(p, a, half))
                    part = slice(2 * P * half, 2 * P * (half + 1))
                    nc.vector.scalar_tensor_tensor(vt_lo[:, :, part],
                                                   gather_bank(p, half)[:].rearrange("p (k t) -> p k t", k=KC),
                                                   1.0 / (HSCALE * PSCALE), vt_hi[:, :, part].bitcast(F32),
                                                   ALU.mult, ALU.subtract).then_inc(vt_lo_ready, 1)

                def attend(p, a, half):
                    dve.wait_ge(attend_done, per_chunk(p, a, half))
                    dve.wait_ge(row_scale_ready, per_group(p, a))
                    for i in range(2):
                        b = 2 * half + i
                        last = nc.vector.scalar_tensor_tensor(
                            x_res[a][:, b, :], attend_bank(p, half)[:, i * D:(i + 1) * D],
                            row_scale[a][:, b:b + 1], x_res[a][:, b, :], ALU.mult, ALU.add)
                    last.then_inc(out_ready, 1)

                all_pairs(dve, gate, {
                    "stats_gnn": lambda p, a: stats_gnn(dve, p, a), "split_gnn": lambda p, a: split_gnn(dve, p, a),
                    "stats_att": stats_att,
                    "update": update, "split_state": split_state,
                    "first_transpose": lambda *which: first_transpose_dve(dve, *which),
                    "transpose": transpose, "residual": residual, "split_att": split_att, "dots": dots,
                    "neighbours": lambda *which: neighbours_dve(dve, *which), "gather": gather, "scores": scores,
                    "probs_transpose": probs_transpose, "attend": attend})

            @block.gpsimd
            def _(pool):
                all_pairs(pool, lambda *step: None, {
                    "stats_gnn": lambda p, a: norm_factors(pool, "gnn", p, a, relu_gnn_ready),
                    "stats_att": lambda p, a: norm_factors(pool, "att", p, a, relu_att_ready)})


_INS = ["x", "adj", "L0_gnn_weight", "L0_gnn_w_ih", "L0_gnn_w_hh", "L0_gnn_b_ih", "L0_gnn_b_hh", "L1_gnn_W",
        "L1_gnn_a"]


def kernel(**inputs):
    import numpy as _np
    import concourse.bacc as _bacc
    from concourse import mybir as _mybir
    from concourse.bass_utils import run_bass_kernel_spmd as _run

    nc = _bacc.Bacc("TRN2", target_bir_lowering=False, num_devices=1)
    arrays, args = {}, []
    for name in _INS:
        a = _np.ascontiguousarray(inputs[name])
        arrays[f"in_{name}_dram"] = a
        args.append(nc.dram_tensor(f"in_{name}_dram", a.shape, _mybir.dt.from_np(a.dtype), kind="ExternalInput").ap())
    out = nc.dram_tensor("out_dram", inputs["x"].shape, _mybir.dt.float32, kind="ExternalOutput").ap()
    graph_blocks(nc, *args, out)
    r = _run(nc, [arrays], core_ids=[0])
    return r.results[0]["out_dram"]
```
